# Optimizing a Trainium2 kernel written in Bass

```python
import numpy as np
import jax
import jax.numpy as jnp

def _softmax(x, axis=-1):
    return jax.nn.softmax(x, axis=axis)

def _gelu(x):
    return jax.nn.gelu(x, approximate=True)

def _silu(x):
    return jax.nn.silu(x)

def _sigmoid(x):
    return jax.nn.sigmoid(x)

def _layernorm(x, axis=-1, eps=1e-05):
    m = jnp.mean(x, axis=axis, keepdims=True)
    v = jnp.var(x, axis=axis, keepdims=True)
    return (x - m) / jnp.sqrt(v + eps)

def _scatter_add(tgt, idx, src, axis=0):
    return tgt.at[idx].add(src)

def _segment_sum(src, seg, n):
    return jax.ops.segment_sum(src, seg, n)
kernel_name = 'mk_perceiver_d1_seqx_r8_b33bd4'

def setup_inputs(seed: int=0):
    np.random.seed(seed)
    _w = jnp.asarray

    def _rec_inputs():
        import jax
        import jax.numpy as jnp
        _rk = jax.random.key(seed)
        x = -0.0002928 + 1 * jax.random.normal(jax.random.fold_in(_rk, 1), (4, 128, 128), jnp.float32)
        _lenS = 128 - jax.random.randint(jax.random.fold_in(_rk, 7), (4,), 0, max(1, 128 // 4) + 1, jnp.int32)
        _lenS2 = 2048 - jax.random.randint(jax.random.fold_in(_rk, 8), (4,), 0, max(1, 2048 // 4) + 1, jnp.int32)
        _ctx_1024P = jax.random.normal(jax.random.fold_in(_rk, 11), (4, 16, 128), jnp.float32)
        _ctx_1024c = jax.random.dirichlet(jax.random.fold_in(_rk, 511), 0.3 * jnp.ones((16,), jnp.float32), (4, 2048))
        _ctx_1024t = jnp.einsum('bsk,bkd->bsd', _ctx_1024c, _ctx_1024P)
        _ctx_1024t = _ctx_1024t * jax.lax.rsqrt(jnp.mean(jnp.square(_ctx_1024t)) + 1e-12) * 0.953939
        ctx_1024 = 4.13588e-05 + 0.999923 * (_ctx_1024t + 0.3 * jax.random.normal(jax.random.fold_in(_rk, 611), (4, 2048, 128), jnp.float32))
        return (x, ctx_1024)
    x, ctx_1024 = _rec_inputs()

    def _L0_xattn_setup():
        import jax, jax.numpy as jnp
        import numpy as np
        HIDDEN = 128
        HEADS = 16
        HEAD_DIM = 64
        key = jax.random.key(seed)
        ks = jax.random.split(key, 7)
        B, Q, K = (2, 256, 512)
        s = 1.0 / np.sqrt(HIDDEN)
        return {'query': jax.random.normal(ks[0], (B, Q, HIDDEN), dtype=jnp.float32), 'key': jax.random.normal(ks[1], (B, K, HIDDEN), dtype=jnp.float32), 'value': jax.random.normal(ks[2], (B, K, HIDDEN), dtype=jnp.float32), 'w_q': jax.random.normal(ks[3], (HIDDEN, HEADS * HEAD_DIM), dtype=jnp.float32) * s, 'w_k': jax.random.normal(ks[4], (HIDDEN, HEADS * HEAD_DIM), dtype=jnp.float32) * s, 'w_v': jax.random.normal(ks[5], (HIDDEN, HEADS * HEAD_DIM), dtype=jnp.float32) * s, 'w_o': jax.random.normal(ks[6], (HEADS * HEAD_DIM, HIDDEN), dtype=jnp.float32) * s}
    _L0_xattn_all = _L0_xattn_setup()
    _L0_xattn_in = {k: v for k, v in _L0_xattn_all.items() if k in ('w_q', 'w_k', 'w_v', 'w_o')}
    del _L0_xattn_all

    def _L0_attn_setup():
        import math
        import jax, jax.numpy as jnp
        import numpy as np
        B, L, DIM, HEADS = (4, 256, 128, 8)
        HEAD = DIM // HEADS
        SCALE_BASE = 512.0
        EPS = 1e-05

        def _xpos(x, downscale=False):
            l, dh = (x.shape[-2], x.shape[-1])
            half = dh // 2
            pos = jnp.arange(l, dtype=x.dtype)
            base = (jnp.arange(0, dh, 2, dtype=x.dtype) + 0.4 * dh) / (1.4 * dh)
            scale = base[None, :] ** (pos[:, None] / SCALE_BASE)
            inv_freq = 1.0 / 10000.0 ** (jnp.arange(half, dtype=x.dtype) / half)
            sinusoid = pos[:, None] * inv_freq[None, :]
            sin, cos = (jnp.sin(sinusoid), jnp.cos(sinusoid))
            if downscale:
                scale = 1.0 / scale
            s = jnp.repeat(sin * scale, 2, axis=-1)
            c = jnp.repeat(cos * scale, 2, axis=-1)
            x1, x2 = (x[..., ::2], x[..., 1::2])
            rot = jnp.stack([-x2, x1], axis=-1).reshape(x.shape)
            return x * c + rot * s

        def _decay_mask(l, gammas):
            n = jnp.arange(l)[:, None]
            m = jnp.arange(l)[None, :]
            lg = jnp.log(gammas)
            expo = (n - m).astype(jnp.float32)[None, :, :] * lg[:, None, None]
            return jnp.where((n >= m)[None], jnp.exp(expo), 0.0)
        key = jax.random.key(seed)
        ks = jax.random.split(key, 6)
        d = DIM
        return {'X': jax.random.normal(ks[0], (B, L, DIM), dtype=jnp.float32), 'W_Q': jax.random.normal(ks[1], (HEADS, DIM, HEAD), dtype=jnp.float32) / d, 'W_K': jax.random.normal(ks[2], (HEADS, DIM, HEAD), dtype=jnp.float32) / d, 'W_V': jax.random.normal(ks[3], (HEADS, DIM, HEAD), dtype=jnp.float32) / d, 'W_G': jax.random.normal(ks[4], (DIM, DIM), dtype=jnp.float32) / d, 'W_O': jax.random.normal(ks[5], (DIM, DIM), dtype=jnp.float32) / d, 'gn_weight': jnp.ones((DIM,), dtype=jnp.float32), 'gn_bias': jnp.zeros((DIM,), dtype=jnp.float32)}
    _L0_attn_all = _L0_attn_setup()
    _L0_attn_in = {k: v for k, v in _L0_attn_all.items() if k in ('W_Q', 'W_K', 'W_V', 'W_G', 'W_O', 'gn_weight', 'gn_bias')}
    del _L0_attn_all

    def _L0_ffn_setup():
        import jax, jax.numpy as jnp
        import numpy as np
        D = 128
        LW = 16
        DEPTH = 8
        NN = 2 ** DEPTH - 1
        NL = 2 ** DEPTH
        B, S = (2, 128)

        def _fff(x, nw, nb, w1, b1, w2, b2, act):
            node = jnp.zeros(x.shape[:2], dtype=jnp.int32)
            for _ in range(DEPTH):
                logit = jnp.einsum('bsd,bsd->bs', x, nw[node]) + nb[node]
                node = 2 * node + 1 + (logit > 0).astype(jnp.int32)
            leaf = node - NN
            h = act(jnp.einsum('bsd,bsdl->bsl', x, w1[leaf]) + b1[leaf])
            return jnp.einsum('bsl,bsld->bsd', h, w2[leaf]) + b2[leaf]

        def _forward(x, q_nw, q_nb, q_w1, q_b1, q_w2, q_b2, k_nw, k_nb, k_w1, k_b1, k_w2, k_b2, v_nw, v_nb, v_w1, v_b1, v_w2, v_b2, f_nw, f_nb, f_w1, f_b1, f_w2, f_b2):
            mu = jnp.mean(x, -1, keepdims=True)
            sd = jnp.std(x, -1, ddof=1, keepdims=True)
            xn = (x - mu) / jnp.sqrt(sd + 1e-05)
            relu = jax.nn.relu
            q = _fff(xn, q_nw, q_nb, q_w1, q_b1, q_w2, q_b2, relu)
            k = _fff(xn, k_nw, k_nb, k_w1, k_b1, k_w2, k_b2, relu)
            v = _fff(xn, v_nw, v_nb, v_w1, v_b1, v_w2, v_b2, relu)
            att = jax.nn.softmax(jnp.einsum('bqd,bkd->bqk', q, k) / jnp.sqrt(jnp.float32(D)), axis=-1)
            y = xn + jnp.einsum('bqk,bkd->bqd', att, v)
            gelu = lambda t: jax.nn.gelu(t, approximate=False)
            return y + _fff(y, f_nw, f_nb, f_w1, f_b1, f_w2, f_b2, gelu)

        def _make_fff_params(key, scale_in, scale_leaf):
            ks = jax.random.split(key, 4)
            nw = jax.random.normal(ks[0], (NN, D), jnp.float32) * scale_in
            nb = jnp.zeros((NN,), jnp.float32)
            w1 = jax.random.normal(ks[1], (NL, D, LW), jnp.float32) * scale_in
            b1 = jax.random.normal(ks[2], (NL, LW), jnp.float32) * 0.01
            w2 = jax.random.normal(ks[3], (NL, LW, D), jnp.float32) * scale_leaf
            b2 = jnp.zeros((NL, D), jnp.float32)
            return (nw, nb, w1, b1, w2, b2)
        key = jax.random.key(seed)
        kx, kq, kk, kv, kf = jax.random.split(key, 5)
        s_in = 1.0 / np.sqrt(D)
        s_lf = 1.0 / np.sqrt(LW)
        inp = {'x': jax.random.normal(kx, (B, S, D), jnp.float32)}
        for name, kk_ in (('q', kq), ('k', kk), ('v', kv), ('f', kf)):
            nw, nb, w1, b1, w2, b2 = _make_fff_params(kk_, s_in, s_lf)
            inp.update({f'{name}_nw': nw, f'{name}_nb': nb, f'{name}_w1': w1, f'{name}_b1': b1, f'{name}_w2': w2, f'{name}_b2': b2})
        return inp
    _L0_ffn_all = _L0_ffn_setup()
    _L0_ffn_in = {k: v for k, v in _L0_ffn_all.items() if k in ('q_nw', 'q_nb', 'q_w1', 'q_b1', 'q_w2', 'q_b2', 'k_nw', 'k_nb', 'k_w1', 'k_b1', 'k_w2', 'k_b2', 'v_nw', 'v_nb', 'v_w1', 'v_b1', 'v_w2', 'v_b2', 'f_nw', 'f_nb', 'f_w1', 'f_b1', 'f_w2', 'f_b2')}
    del _L0_ffn_all
    return {'x': x, 'ctx_1024': ctx_1024, 'L0_xattn_w_q': _L0_xattn_in['w_q'], 'L0_xattn_w_k': _L0_xattn_in['w_k'], 'L0_xattn_w_v': _L0_xattn_in['w_v'], 'L0_xattn_w_o': _L0_xattn_in['w_o'], 'L0_attn_W_Q': _L0_attn_in['W_Q'], 'L0_attn_W_K': _L0_attn_in['W_K'], 'L0_attn_W_V': _L0_attn_in['W_V'], 'L0_attn_W_G': _L0_attn_in['W_G'], 'L0_attn_W_O': _L0_attn_in['W_O'], 'L0_attn_gn_weight': _L0_attn_in['gn_weight'], 'L0_attn_gn_bias': _L0_attn_in['gn_bias'], 'L0_ffn_q_nw': _L0_ffn_in['q_nw'], 'L0_ffn_q_nb': _L0_ffn_in['q_nb'], 'L0_ffn_q_w1': _L0_ffn_in['q_w1'], 'L0_ffn_q_b1': _L0_ffn_in['q_b1'], 'L0_ffn_q_w2': _L0_ffn_in['q_w2'], 'L0_ffn_q_b2': _L0_ffn_in['q_b2'], 'L0_ffn_k_nw': _L0_ffn_in['k_nw'], 'L0_ffn_k_nb': _L0_ffn_in['k_nb'], 'L0_ffn_k_w1': _L0_ffn_in['k_w1'], 'L0_ffn_k_b1': _L0_ffn_in['k_b1'], 'L0_ffn_k_w2': _L0_ffn_in['k_w2'], 'L0_ffn_k_b2': _L0_ffn_in['k_b2'], 'L0_ffn_v_nw': _L0_ffn_in['v_nw'], 'L0_ffn_v_nb': _L0_ffn_in['v_nb'], 'L0_ffn_v_w1': _L0_ffn_in['v_w1'], 'L0_ffn_v_b1': _L0_ffn_in['v_b1'], 'L0_ffn_v_w2': _L0_ffn_in['v_w2'], 'L0_ffn_v_b2': _L0_ffn_in['v_b2'], 'L0_ffn_f_nw': _L0_ffn_in['f_nw'], 'L0_ffn_f_nb': _L0_ffn_in['f_nb'], 'L0_ffn_f_w1': _L0_ffn_in['f_w1'], 'L0_ffn_f_b1': _L0_ffn_in['f_b1'], 'L0_ffn_f_w2': _L0_ffn_in['f_w2'], 'L0_ffn_f_b2': _L0_ffn_in['f_b2']}

def reference(x, ctx_1024, L0_xattn_w_q, L0_xattn_w_k, L0_xattn_w_v, L0_xattn_w_o, L0_attn_W_Q, L0_attn_W_K, L0_attn_W_V, L0_attn_W_G, L0_attn_W_O, L0_attn_gn_weight, L0_attn_gn_bias, L0_ffn_q_nw, L0_ffn_q_nb, L0_ffn_q_w1, L0_ffn_q_b1, L0_ffn_q_w2, L0_ffn_q_b2, L0_ffn_k_nw, L0_ffn_k_nb, L0_ffn_k_w1, L0_ffn_k_b1, L0_ffn_k_w2, L0_ffn_k_b2, L0_ffn_v_nw, L0_ffn_v_nb, L0_ffn_v_w1, L0_ffn_v_b1, L0_ffn_v_w2, L0_ffn_v_b2, L0_ffn_f_nw, L0_ffn_f_nb, L0_ffn_f_w1, L0_ffn_f_b1, L0_ffn_f_w2, L0_ffn_f_b2):
    import jax
    import jax.numpy as jnp

    def _L0_xattn_ref(query, key, value, w_q, w_k, w_v, w_o):
        import jax, jax.numpy as jnp
        import numpy as np
        HIDDEN = 128
        HEADS = 16
        HEAD_DIM = 64
        B, Q, _ = query.shape
        Kl = key.shape[1]
        scale = HEAD_DIM ** (-0.5)
        q = (query @ w_q).reshape(B, Q, HEADS, HEAD_DIM).transpose(0, 2, 1, 3)
        k = (key @ w_k).reshape(B, Kl, HEADS, HEAD_DIM).transpose(0, 2, 1, 3)
        v = (value @ w_v).reshape(B, Kl, HEADS, HEAD_DIM).transpose(0, 2, 1, 3)
        scores = jnp.einsum('bhqd,bhkd->bhqk', q, k) * scale
        attn = jax.nn.softmax(scores, axis=-1)
        out = jnp.einsum('bhqk,bhkd->bhqd', attn, v)
        out = out.transpose(0, 2, 1, 3).reshape(B, Q, HEADS * HEAD_DIM)
        return out @ w_o

    def _L0_attn_ref(X, W_Q, W_K, W_V, W_G, W_O, gn_weight, gn_bias):
        import math
        import jax, jax.numpy as jnp
        import numpy as np
        B, L, DIM, HEADS = (4, 256, 128, 8)
        HEAD = DIM // HEADS
        SCALE_BASE = 512.0
        EPS = 1e-05

        def _xpos(x, downscale=False):
            l, dh = (x.shape[-2], x.shape[-1])
            half = dh // 2
            pos = jnp.arange(l, dtype=x.dtype)
            base = (jnp.arange(0, dh, 2, dtype=x.dtype) + 0.4 * dh) / (1.4 * dh)
            scale = base[None, :] ** (pos[:, None] / SCALE_BASE)
            inv_freq = 1.0 / 10000.0 ** (jnp.arange(half, dtype=x.dtype) / half)
            sinusoid = pos[:, None] * inv_freq[None, :]
            sin, cos = (jnp.sin(sinusoid), jnp.cos(sinusoid))
            if downscale:
                scale = 1.0 / scale
            s = jnp.repeat(sin * scale, 2, axis=-1)
            c = jnp.repeat(cos * scale, 2, axis=-1)
            x1, x2 = (x[..., ::2], x[..., 1::2])
            rot = jnp.stack([-x2, x1], axis=-1).reshape(x.shape)
            return x * c + rot * s

        def _decay_mask(l, gammas):
            n = jnp.arange(l)[:, None]
            m = jnp.arange(l)[None, :]
            lg = jnp.log(gammas)
            expo = (n - m).astype(jnp.float32)[None, :, :] * lg[:, None, None]
            return jnp.where((n >= m)[None], jnp.exp(expo), 0.0)
        b, l, d = X.shape
        h = W_Q.shape[0]
        gammas = 1.0 - jnp.exp(jnp.linspace(math.log(1.0 / 32.0), math.log(1.0 / 512.0), h)).astype(jnp.float32)
        Q = jnp.einsum('bld,hde->bhle', X, W_Q)
        K = jnp.einsum('bld,hde->bhle', X, W_K)
        V = jnp.einsum('bld,hdv->bhlv', X, W_V)
        Q = _xpos(Q)
        K = _xpos(K, downscale=True)
        D = _decay_mask(l, gammas).astype(X.dtype)
        scores = jnp.einsum('bhle,bhme->bhlm', Q, K) * D[None]
        Y = jnp.einsum('bhlm,bhmv->bhlv', scores, V)
        mean = Y.mean(axis=-1, keepdims=True)
        var = Y.var(axis=-1, keepdims=True)
        Yn = (Y - mean) * jax.lax.rsqrt(var + EPS)
        Yn = jnp.transpose(Yn, (0, 2, 1, 3)).reshape(b, l, -1)
        Yn = Yn * gn_weight + gn_bias
        G = X @ W_G
        out = G * jax.nn.sigmoid(G) * Yn @ W_O
        return out

    def _L0_ffn_ref(x, q_nw, q_nb, q_w1, q_b1, q_w2, q_b2, k_nw, k_nb, k_w1, k_b1, k_w2, k_b2, v_nw, v_nb, v_w1, v_b1, v_w2, v_b2, f_nw, f_nb, f_w1, f_b1, f_w2, f_b2):
        import jax, jax.numpy as jnp
        import numpy as np
        D = 128
        LW = 16
        DEPTH = 8
        NN = 2 ** DEPTH - 1
        NL = 2 ** DEPTH
        B, S = (2, 128)

        def _fff(x, nw, nb, w1, b1, w2, b2, act):
            node = jnp.zeros(x.shape[:2], dtype=jnp.int32)
            for _ in range(DEPTH):
                logit = jnp.einsum('bsd,bsd->bs', x, nw[node]) + nb[node]
                node = 2 * node + 1 + (logit > 0).astype(jnp.int32)
            leaf = node - NN
            h = act(jnp.einsum('bsd,bsdl->bsl', x, w1[leaf]) + b1[leaf])
            return jnp.einsum('bsl,bsld->bsd', h, w2[leaf]) + b2[leaf]

        def _forward(x, q_nw, q_nb, q_w1, q_b1, q_w2, q_b2, k_nw, k_nb, k_w1, k_b1, k_w2, k_b2, v_nw, v_nb, v_w1, v_b1, v_w2, v_b2, f_nw, f_nb, f_w1, f_b1, f_w2, f_b2):
            mu = jnp.mean(x, -1, keepdims=True)
            sd = jnp.std(x, -1, ddof=1, keepdims=True)
            xn = (x - mu) / jnp.sqrt(sd + 1e-05)
            relu = jax.nn.relu
            q = _fff(xn, q_nw, q_nb, q_w1, q_b1, q_w2, q_b2, relu)
            k = _fff(xn, k_nw, k_nb, k_w1, k_b1, k_w2, k_b2, relu)
            v = _fff(xn, v_nw, v_nb, v_w1, v_b1, v_w2, v_b2, relu)
            att = jax.nn.softmax(jnp.einsum('bqd,bkd->bqk', q, k) / jnp.sqrt(jnp.float32(D)), axis=-1)
            y = xn + jnp.einsum('bqk,bkd->bqd', att, v)
            gelu = lambda t: jax.nn.gelu(t, approximate=False)
            return y + _fff(y, f_nw, f_nb, f_w1, f_b1, f_w2, f_b2, gelu)

        def _make_fff_params(key, scale_in, scale_leaf):
            ks = jax.random.split(key, 4)
            nw = jax.random.normal(ks[0], (NN, D), jnp.float32) * scale_in
            nb = jnp.zeros((NN,), jnp.float32)
            w1 = jax.random.normal(ks[1], (NL, D, LW), jnp.float32) * scale_in
            b1 = jax.random.normal(ks[2], (NL, LW), jnp.float32) * 0.01
            w2 = jax.random.normal(ks[3], (NL, LW, D), jnp.float32) * scale_leaf
            b2 = jnp.zeros((NL, D), jnp.float32)
            return (nw, nb, w1, b1, w2, b2)
        return _forward(x, q_nw, q_nb, q_w1, q_b1, q_w2, q_b2, k_nw, k_nb, k_w1, k_b1, k_w2, k_b2, v_nw, v_nb, v_w1, v_b1, v_w2, v_b2, f_nw, f_nb, f_w1, f_b1, f_w2, f_b2)
    x = x + _L0_xattn_ref(_layernorm(x, axis=-1), ctx_1024, ctx_1024, L0_xattn_w_q, L0_xattn_w_k, L0_xattn_w_v, L0_xattn_w_o)
    x = x + _L0_attn_ref(_layernorm(x, axis=-1), L0_attn_W_Q, L0_attn_W_K, L0_attn_W_V, L0_attn_W_G, L0_attn_W_O, L0_attn_gn_weight, L0_attn_gn_bias)
    x = x + _L0_ffn_ref(_layernorm(x, axis=-1), L0_ffn_q_nw, L0_ffn_q_nb, L0_ffn_q_w1, L0_ffn_q_b1, L0_ffn_q_w2, L0_ffn_q_b2, L0_ffn_k_nw, L0_ffn_k_nb, L0_ffn_k_w1, L0_ffn_k_b1, L0_ffn_k_w2, L0_ffn_k_b2, L0_ffn_v_nw, L0_ffn_v_nb, L0_ffn_v_w1, L0_ffn_v_b1, L0_ffn_v_w2, L0_ffn_v_b2, L0_ffn_f_nw, L0_ffn_f_nb, L0_ffn_f_w1, L0_ffn_f_b1, L0_ffn_f_w2, L0_ffn_f_b2)
    return x

_drawn_inputs = setup_inputs


def setup_inputs(seed=0):
    import zlib

    import numpy as np

    out = dict(_drawn_inputs(seed))
    spreads = {'L0_attn_gn_weight': (1.0, 0.2),
     'L0_attn_gn_bias': (0.0, 1.734),
     'L0_ffn_q_nb': (0.0, 0.1),
     'L0_ffn_q_b2': (0.0, 0.303),
     'L0_ffn_k_nb': (0.0, 0.1),
     'L0_ffn_k_b2': (0.0, 0.1),
     'L0_ffn_v_nb': (0.0, 0.1),
     'L0_ffn_v_b2': (0.0, 0.1),
     'L0_ffn_f_nb': (0.0, 0.1),
     'L0_ffn_f_b2': (0.0, 0.1)}
    factors = {'L0_ffn_q_b1': 8.0, 'L0_ffn_k_b1': 4.839, 'L0_ffn_v_b1': 2.728, 'L0_ffn_f_b1': 25.764}
    for name, (base, spread) in spreads.items():
        noise = np.random.default_rng([zlib.crc32(name.encode()), seed]).standard_normal(out[name].shape)
        drawn = base * np.exp(spread * noise) if base else spread * noise
        out[name] = jnp.asarray(drawn.astype(out[name].dtype))
    for name, factor in factors.items():
        out[name] = (out[name] * factor).astype(out[name].dtype)
    return out
```

```python
import concourse.bass as bass
from concourse import mybir
from contextlib import ExitStack

F32 = mybir.dt.float32
F32R = mybir.dt.float32r
I32 = mybir.dt.int32
ALU = mybir.AluOpType
ACT = mybir.ActivationFunctionType
AXX = mybir.AxisListType.X

P = 128
D = 128
B = 4
NK = 2048
H, DH = 16, 64
HEADS = B * H
PAIRS = HEADS // 2
PPB = H // 2
KT = NK // P
CH = 4
KPC = KT // CH
RH, RE = 8, 16
LEAVES, NODES, DEPTH, LW = 256, 255, 8, 16
W1 = D * LW
ROW = 2 * W1 + LW + D
EPS = 1e-5
QSCALE = DH ** -0.5
FSCALE = D ** -0.5

PHASE_AT = [(21, 0), (21, 1), (22, 0), (22, 1), (23, 0), (23, 1), (24, 0), (25, 0), (25, 1), (26, 1),
            (27, 0), (27, 1), (28, 1), (29, 1), (30, 1), (31, 1), (32, 1), (33, 0), (33, 1), (34, 0),
            (34, 1), (35, 0), (36, 0), (36, 1)]
SLOTS = H * (B - 1) + PHASE_AT[-1][0] + 1


def phases_at(slot, place):
    return [(k, b) for b in range(B) for k, (s, p) in enumerate(PHASE_AT) if H * b + s == slot and p == place]


def ring_items(slot):
    out = [("T", slot - 2, g) for g in range(CH)] if 0 <= slot - 2 < HEADS else []
    if slot % 2:
        if (slot + 1) // 2 < PAIRS or 0 <= (slot - 5) // 2 < PAIRS:
            out.append(("QO", slot, 0))
    elif 0 <= (slot - 6) // 2 < PAIRS:
        out.append(("OT", slot, 0))
    return out


RING = {}
for _slot in range(SLOTS):
    for _item in ring_items(_slot):
        RING[_item] = len(RING)


def program(nc, x, ctx_rows, ctx_t, wq_t, wk_t, w_v, w_o, w_small, xpos, decay, head_mask, gn_wb, node_w,
            node_b, leaves, leaf_ids, ident_in, out):
    es = ExitStack()
    with es:
        def sb(name, shape, dt=F32):
            return es.enter_context(nc.sbuf_tensor(name, shape, dt))

        def pb(name, shape):
            return es.enter_context(nc.psum_tensor(name, shape, F32))

        def sem(name):
            return es.enter_context(nc.semaphore(name))

        ct_stage = sb("ct_stage", [P, 2, 512])
        c_stage = sb("c_stage", [P, 2, KPC, D])
        ct_hi, ct_lo = sb("ct_hi", [P, NK], F32R), sb("ct_lo", [P, NK], F32R)
        c_hi, c_lo = sb("c_hi", [P, KT, D], F32R), sb("c_lo", [P, KT, D], F32R)
        prob = sb("prob", [P, 2, NK])
        pt_hi = sb("pt_hi", [P, 3, KT // 2, 2 * P], F32R)
        pt_lo = sb("pt_lo", [P, 3, KT // 2, 2 * P], F32R)
        q_hi, q_lo = sb("q_hi", [P, 2, 2 * P], F32R), sb("q_lo", [P, 2, 2 * P], F32R)
        wqk = sb("wqk", [P, H, D])
        wv = sb("wv", [P, H * DH])
        wo = sb("wo", [P, PPB, D])
        x_sb = sb("x_sb", [P, B, D])
        xn_t = sb("xn_t", [P, B, P])
        av_sb = sb("av_sb", [P, 2 * P])
        o_sb = sb("o_sb", [P, 2, DH])
        ot_sb = sb("ot_sb", [P, PPB, P])
        chunk_max = sb("chunk_max", [P, HEADS, 2])
        neg_max = sb("neg_max", [P, HEADS])
        sums = sb("sums", [P, HEADS, 2])
        sum_all = sb("sum_all", [P, HEADS])
        rsum = sb("rsum", [P, HEADS])
        ident = sb("ident", [P, P])
        wsm = sb("wsm", [P, 7, D])
        xp = sb("xp", [P, 4, P])
        dec = sb("dec", [P, RH, P])
        hmask = sb("hmask", [P, RH])
        gn = sb("gn", [P, 2, D])
        nw = sb("nw", [P, 4, NODES])
        nb = sb("nb", [P, 4, NODES])
        lid = sb("lid", [P, 2, LEAVES // 2])
        st6 = sb("st6", [P, B, 6])
        mv = sb("mv", [P, B, 2])
        var = sb("var", [P, RH])
        rstd = sb("rstd", [P, RH])
        half = sb("half", [P, 2, RH])
        x1, x2, xf, y = sb("x1", [P, D]), sb("x2", [P, D]), sb("xf", [P, D]), sb("y", [P, D])
        xn1, tr_sb = sb("xn1", [P, D]), sb("tr_sb", [P, 2, P])
        qk_a, qk_b, qk_x = sb("qk_a", [P, 2, P]), sb("qk_b", [P, 2, P]), sb("qk_x", [P, 2, P])
        xl = qk_b[:, 0, :]
        v_sb, silu = sb("v_sb", [P, D]), sb("silu", [P, D])
        qmask = sb("qmask", [P, RH, P])
        sm = qmask
        gmean = sb("gmean", [P, RH])
        yc, ysq = qk_a[:, 0, :], qk_a[:, 1, :]
        right = sb("right", [P, 3, NODES], I32)
        cur = sb("cur", [P, 3, LEAVES // 2])
        idx = sb("idx", [P, 4], I32)
        leaf = [sb("leaf0", [P, ROW]), sb("leaf1", [P, ROW])]
        hid = sb("hid", [P, LW])
        tree = sb("tree", [P, 4, D])
        att_nm, att_sum, att_r = sb("att_nm", [P, 1]), sb("att_sum", [P, 1]), sb("att_r", [P, 1])
        att_p = xn1
        res = sb("res", [P, D])

        ps_s = pb("ps_s", [P, NK])
        ps_ring = pb("ps_ring", [P, 2, 512])
        ps_av = pb("ps_av", [P, 512])
        ps_m = pb("ps_m", [P, 512])

        names = """ld_x ld_wqk ld_ct0 ld_ct1 ld_c0 ld_c1 ld_wvo ld_rest gather0 gather1 stored
            var_ready rstd_ready xn_ready xnt_done xnt_ready wqk_done wqk_a wqk_b q0_done q0_ready
            ct_split c_split s_done negmax_ready exp_done ring_filled ring_free hi_done av_done av_taken
            dve_link pool_link proj_done xn1_ready xn1t_done tr_ready qk_done qkx_ready qmask_ready vg_done
            v_ready eg_ready silu_ready sc_done sm_ready y_done gated_ready gatedt_done wo_done xf_ready
            xft_done lg_done mask_ready lgv_done idx_ready prod_ready h_ready leaf_taken ff_pre
            qkt_done at_done nm_ready ap_ready apt_done yv_done y_ready yt_done lgf_done idxf_ready
            out_ready""".split()
        S = {n: sem(n) for n in names}
        block = es.enter_context(nc.Block())

        def part(pair, kt):
            return (0, kt) if kt < KT // 2 else (1 + pair % 2, kt - KT // 2)

        def wqk_at(h):
            return (h % 2) * (H // 2) + h // 2

        def pows(b, i):
            return 2 + 4 * b + i

        def prods(b, tree_no, step):
            return 8 * b + 2 * tree_no + step + 1

        def store(sp, b):
            sp.wait_ge(S["out_ready"], b + 1)
            sp.dma_start(out[b], res[:]).then_inc(S["stored"], 16)

        @block.sync
        def _(sp):
            def load_ct(i):
                if i >= 2:
                    sp.wait_ge(S["ct_split"], i - 1)
                sp.dma_start(ct_stage[:, i % 2, :], ctx_t[i // CH, :, 512 * (i % CH):512 * (i % CH + 1)])\
                    .then_inc(S[f"ld_ct{i % 2}"], 16)

            def load_c(i):
                if i >= 2:
                    sp.wait_ge(S["c_split"], i - 1)
                rows = ctx_rows[i // CH, 512 * (i % CH):512 * (i % CH + 1), :]
                sp.dma_start(c_stage[:, i % 2, :, :], rows.rearrange("(k p) d -> p k d", p=P))\
                    .then_inc(S[f"ld_c{i % 2}"], 16)

            sp.dma_start(x_sb[:], x.rearrange("b p d -> p b d")).then_inc(S["ld_x"], 16)
            load_ct(0)
            load_ct(1)
            sp.dma_start(wv[:], w_v).then_inc(S["ld_wvo"], 16)
            sp.dma_start(wo[:], w_o.rearrange("(i p) n -> p i n", p=P)).then_inc(S["ld_wvo"], 16)
            load_ct(2)
            load_ct(3)
            load_c(0)
            load_c(1)
            sp.dma_start(wsm[:], w_small).then_inc(S["ld_rest"], 16)
            sp.dma_start(xp[:], xpos).then_inc(S["ld_rest"], 16)
            sp.dma_start(dec[:], decay).then_inc(S["ld_rest"], 16)
            sp.dma_start(hmask[:], head_mask).then_inc(S["ld_rest"], 16)
            sp.dma_start(gn[:], gn_wb.partition_broadcast(P)).then_inc(S["ld_rest"], 16)
            sp.dma_start(nw[:], node_w).then_inc(S["ld_rest"], 16)
            sp.dma_start(nb[:], node_b.partition_broadcast(P)).then_inc(S["ld_rest"], 16)
            sp.dma_start(lid[:], leaf_ids.partition_broadcast(P)).then_inc(S["ld_rest"], 16)
            load_c(2)
            load_c(3)
            for b in range(B):
                if b + 1 < B:
                    for c in range(CH):
                        load_ct(CH * (b + 1) + c)
                    for c in range(CH):
                        load_c(CH * (b + 1) + c)
                if b >= 1:
                    store(sp, b - 1)
            store(sp, B - 1)
            sp.wait_ge(S["stored"], 16 * B)

        @block.tensor
        def _(pe):
            def mm(o, l, r, start=True, stop=True):
                return nc.tensor.matmul(o, l, r, start=start, stop=stop)

            def ring_slot(item):
                i = RING[item]
                if i >= 2:
                    pe.wait_ge(S["ring_free"], i - 1)
                return ps_ring[:, i % 2, :]

            def rest(k, b):
                if k == 0:
                    pe.wait_ge(S["ring_free"], RING[("OT", H * b + 2 * (PPB - 1) + 6, 0)] + 1)
                    if b >= 1:
                        pe.wait_ge(S["idxf_ready"], b)
                    for i in range(PPB):
                        last = mm(ps_m[:, 0:P], ot_sb[:, i, :], wo[:, i, :], i == 0, i == PPB - 1)
                    last.then_inc(S["proj_done"], 1)
                elif k == 1:
                    pe.wait_ge(S["xn1_ready"], b + 1)
                    nc.tensor.transpose(ps_m[:, P:2 * P], xn1[:], ident[:]).then_inc(S["xn1t_done"], 1)
                elif k == 2:
                    pe.wait_ge(S["tr_ready"], 6 * b + 1)
                    for i in range(4):
                        last = mm(ps_m[:, i * P:(i + 1) * P], wsm[:, i, :], tr_sb[:, 0, :])
                    last.then_inc(S["qk_done"], 1)
                elif k == 3:
                    pe.wait_ge(S["qkx_ready"], b + 1)
                    mm(ps_m[:, 0:P], tr_sb[:, 0, :], wsm[:, 4, :])
                    mm(ps_m[:, P:2 * P], tr_sb[:, 0, :], wsm[:, 5, :]).then_inc(S["vg_done"], 1)
                elif k in (4, 5):
                    if k == 4:
                        pe.wait_ge(S["qmask_ready"], b + 1)
                        pe.wait_ge(S["v_ready"], b + 1)
                        pe.wait_ge(S["silu_ready"], b + 1)
                    else:
                        pe.wait_ge(S["sm_ready"], 2 * b + 1)
                    mm(ps_m[:], qk_x[:, 1, :], qmask[:, 4 * (k - 4):4 * (k - 3), :]).then_inc(S["sc_done"], 1)
                elif k == 6:
                    pe.wait_ge(S["sm_ready"], 2 * b + 2)
                    for h in range(RH):
                        last = mm(ps_m[:, RE * h:RE * (h + 1)], sm[:, h, :], v_sb[:, RE * h:RE * (h + 1)])
                    last.then_inc(S["y_done"], 1)
                elif k == 7:
                    pe.wait_ge(S["gated_ready"], b + 1)
                    nc.tensor.transpose(ps_m[:, P:2 * P], yc, ident[:]).then_inc(S["gatedt_done"], 1)
                elif k == 8:
                    pe.wait_ge(S["tr_ready"], 6 * b + 2)
                    mm(ps_m[:, 2 * P:3 * P], tr_sb[:, 1, :], wsm[:, 6, :]).then_inc(S["wo_done"], 1)
                elif k == 9:
                    pe.wait_ge(S["xf_ready"], b + 1)
                    nc.tensor.transpose(ps_m[:, 0:P], xf[:], ident[:]).then_inc(S["xft_done"], 1)
                elif k == 10:
                    pe.wait_ge(S["tr_ready"], 6 * b + 3)
                    mm(ps_m[:, 0:NODES], tr_sb[:, 0, :], nw[:, 0, :])
                    mm(ps_m[:, 256:256 + NODES], tr_sb[:, 0, :], nw[:, 1, :]).then_inc(S["lg_done"], 1)
                elif k == 11:
                    pe.wait_ge(S["mask_ready"], b + 1)
                    mm(ps_m[:, 0:NODES], tr_sb[:, 0, :], nw[:, 2, :]).then_inc(S["lgv_done"], 1)
                elif k == 16:
                    pe.wait_ge(S["leaf_taken"], 4 * b + 3)
                    nc.tensor.transpose(ps_m[:, 0:P], tree[:, 0, :], ident[:])
                    nc.tensor.transpose(ps_m[:, P:2 * P], tree[:, 1, :], ident[:]).then_inc(S["qkt_done"], 1)
                elif k == 17:
                    pe.wait_ge(S["tr_ready"], 6 * b + 4)
                    mm(ps_m[:, 2 * P:3 * P], tr_sb[:, 0, :], tr_sb[:, 1, :]).then_inc(S["at_done"], 1)
                elif k == 18:
                    pe.wait_ge(S["ap_ready"], b + 1)
                    nc.tensor.transpose(ps_m[:, 3 * P:4 * P], att_p[:], ident[:]).then_inc(S["apt_done"], 1)
                elif k == 19:
                    pe.wait_ge(S["tr_ready"], 6 * b + 5)
                    mm(ps_m[:, 0:P], tr_sb[:, 0, :], tree[:, 2, :]).then_inc(S["yv_done"], 1)
                elif k == 20:
                    pe.wait_ge(S["y_ready"], b + 1)
                    nc.tensor.transpose(ps_m[:, P:2 * P], y[:], ident[:]).then_inc(S["yt_done"], 1)
                elif k == 21:
                    pe.wait_ge(S["tr_ready"], 6 * b + 6)
                    mm(ps_m[:, 256:256 + NODES], tr_sb[:, 1, :], nw[:, 3, :]).then_inc(S["lgf_done"], 1)

            def scores(n, c):
                b, h = n // H, n % H
                if h == 0:
                    pe.wait_ge(S["ct_split"], CH * b + c + 1)
                if n == 0 and c == 0:
                    pe.wait_ge(S["q0_ready"], 1)
                elif n % 2 == 0 and c == 0:
                    pe.wait_ge(S["ring_free"], RING[("QO", n - 1, 0)] + 1)
                if n >= 1 and c % 2 == 0:
                    pe.wait_ge(S["exp_done"], 2 * (n - 1) + c // 2 + 1)
                o = ps_s[:, 512 * c:512 * (c + 1)]
                j = (n // 2) % 2
                qh, ql = q_hi[:, j, P * (n % 2):P * (n % 2 + 1)], q_lo[:, j, P * (n % 2):P * (n % 2 + 1)]
                kh, kl = ct_hi[:, 512 * c:512 * (c + 1)], ct_lo[:, 512 * c:512 * (c + 1)]
                mm(o, qh, kh, True, False)
                mm(o, qh, kl, False, False)
                mm(o, ql, kh, False, True).then_inc(S["s_done"], 1)

            def transposes(n, g):
                pe.wait_ge(S["exp_done"], 2 * n + g // 2 + 1)
                o = ring_slot(("T", n, g))
                for i in range(KPC):
                    k = (KPC * g + i) * P
                    last = nc.tensor.transpose(o[:, i * P:(i + 1) * P], prob[:, n % 2, k:k + P], ident[:])
                last.then_inc(S["ring_filled"], 1)

            def context_half(pair, half_no):
                b = pair // PPB
                pe.wait_ge(S["ring_free"], RING[("T", 2 * pair + 1, 2 * half_no + 1)] + 1)
                if pair % PPB == 0:
                    pe.wait_ge(S["c_split"], CH * b + 2 * (half_no + 1))
                if half_no == 0 and pair >= 1:
                    pe.wait_ge(S["av_taken"], pair)
                for kt in range(8 * half_no, 8 * half_no + 8):
                    pp, row = part(pair, kt)
                    first, end = kt == 0, kt == KT - 1
                    mm(ps_av[:, 0:2 * P], c_hi[:, kt, :], pt_hi[:, pp, row, :], first, False)
                    mm(ps_av[:, 0:2 * P], c_hi[:, kt, :], pt_lo[:, pp, row, :], False, False)
                    last = mm(ps_av[:, 0:2 * P], c_lo[:, kt, :], pt_hi[:, pp, row, :], False, end)
                last.then_inc(S["av_done"], 1)

            def queries(pair, o):
                for j in range(2):
                    last = mm(o[:, j * P:(j + 1) * P], wqk[:, wqk_at((2 * pair + j) % H), :], xn_t[:, pair // PPB, :])
                return last

            pe.wait_ge(S["ld_wqk"], 48)
            for h in range(H):
                r, at = DH * (h % 2), wqk_at(h)
                last = mm(ps_s[:, at * D:(at + 1) * D], prob[r:r + DH, 0, (h // 2) * D:(h // 2 + 1) * D],
                          prob[r:r + DH, 1, (h // 2) * D:(h // 2 + 1) * D])
            last.then_inc(S["wqk_done"], 1)
            pe.wait_ge(S["xn_ready"], 1)
            for t in range(B):
                last = nc.tensor.transpose(ps_m[:, t * P:(t + 1) * P], qmask[:, t, :], ident[:])
            last.then_inc(S["xnt_done"], 1)
            pe.wait_ge(S["wqk_a"], 1)
            pe.wait_ge(S["wqk_b"], 1)
            pe.wait_ge(S["xnt_ready"], 1)
            queries(0, ps_m).then_inc(S["q0_done"], 1)

            for s in range(SLOTS):
                head = s if s < HEADS else None
                tr = s - 2 if 0 <= s - 2 < HEADS else None
                for c in range(CH):
                    if tr is not None and c < 2:
                        transposes(tr, c)
                    if head is not None:
                        scores(head, c)
                    if c == 1:
                        for k, b in phases_at(s, 0):
                            rest(k, b)
                    if tr is not None and c >= 2:
                        transposes(tr, c)
                if ("QO", s, 0) in RING:
                    o = ring_slot(("QO", s, 0))
                    if (s + 1) // 2 < PAIRS:
                        last = queries((s + 1) // 2, o)
                    if 0 <= (s - 5) // 2 < PAIRS:
                        pair = (s - 5) // 2
                        if pair == 0:
                            pe.wait_ge(S["ld_wvo"], 32)
                        pe.wait_ge(S["av_taken"], pair + 1)
                        for j in range(2):
                            h = (2 * pair + j) % H
                            last = mm(o[:, 256 + DH * j:256 + DH * (j + 1)], av_sb[:, j * P:(j + 1) * P],
                                      wv[:, DH * h:DH * (h + 1)])
                    last.then_inc(S["ring_filled"], 1)
                if ("OT", s, 0) in RING:
                    o = ring_slot(("OT", s, 0))
                    pe.wait_ge(S["ring_free"], RING[("QO", s - 1, 0)] + 1)
                    nc.tensor.transpose(o[:, 0:P], o_sb[:].rearrange("p a b -> p (a b)"), ident[:])\
                        .then_inc(S["ring_filled"], 1)
                if s % 2 and 0 <= (s - 3) // 2 < PAIRS:
                    context_half((s - 3) // 2, 0)
                if s % 2 == 0 and 0 <= (s - 4) // 2 < PAIRS:
                    context_half((s - 4) // 2, 1)
                for k, b in phases_at(s, 1):
                    rest(k, b)

        @block.scalar
        def _(act):
            hi_count = [0]

            def rest(k, b):
                if k == 1:
                    act.wait_ge(S["xn1t_done"], b + 1)
                    nc.scalar.copy(tr_sb[:, 0, :], ps_m[:, P:2 * P]).then_inc(S["tr_ready"], 1)
                elif k == 3:
                    act.wait_ge(S["vg_done"], b + 1)
                    nc.scalar.copy(v_sb[:], ps_m[:, 0:P]).then_inc(S["v_ready"], 1)
                    nc.scalar.activation(silu[:], ps_m[:, P:2 * P], ACT.Exp, scale=-1.0).then_inc(S["eg_ready"], 1)
                elif k == 7:
                    act.wait_ge(S["gatedt_done"], b + 1)
                    nc.scalar.copy(tr_sb[:, 1, :], ps_m[:, P:2 * P]).then_inc(S["tr_ready"], 1)
                elif k == 9:
                    act.wait_ge(S["xft_done"], b + 1)
                    nc.scalar.copy(tr_sb[:, 0, :], ps_m[:, 0:P]).then_inc(S["tr_ready"], 1)
                elif k == 16:
                    act.wait_ge(S["qkt_done"], b + 1)
                    nc.scalar.copy(tr_sb[:].rearrange("p a b -> p (a b)"), ps_m[:, 0:2 * P])\
                        .then_inc(S["tr_ready"], 1)
                elif k == 17:
                    act.wait_ge(S["nm_ready"], b + 1)
                    nc.scalar.activation(att_p[:], ps_m[:, 2 * P:3 * P], ACT.Exp, bias=att_nm[:], scale=FSCALE,
                                         accum_out=att_sum[:]).then_inc(S["ap_ready"], 1)
                elif k == 18:
                    act.wait_ge(S["apt_done"], b + 1)
                    nc.scalar.copy(tr_sb[:, 0, :], ps_m[:, 3 * P:4 * P]).then_inc(S["tr_ready"], 1)
                elif k == 20:
                    act.wait_ge(S["yt_done"], b + 1)
                    nc.scalar.copy(tr_sb[:, 1, :], ps_m[:, P:2 * P]).then_inc(S["tr_ready"], 1)
                elif k == 22:
                    act.wait_ge(S["ff_pre"], b + 1)
                    nc.scalar.activation(hid[:], hid[:], ACT.Gelu).then_inc(S["h_ready"], 1)

            act.dma_start(ident[:], ident_in).then_inc(S["ld_wqk"], 16)
            act.dma_start(prob[:, 0, 0:PPB * D].rearrange("p (i d) -> p i d", i=PPB),
                          wq_t.rearrange("(i p) d -> p i d", p=P)).then_inc(S["ld_wqk"], 16)
            act.dma_start(prob[:, 1, 0:PPB * D].rearrange("p (i d) -> p i d", i=PPB),
                          wk_t.rearrange("(i p) d -> p i d", p=P)).then_inc(S["ld_wqk"], 16)
            wqk_flat = wqk[:].rearrange("p h d -> p (h d)")
            act.wait_ge(S["wqk_done"], 1)
            nc.scalar.activation(wqk_flat[:, 0:1024], ps_s[:, 0:1024], ACT.Copy, scale=QSCALE)\
                .then_inc(S["wqk_a"], 1)
            act.wait_ge(S["xnt_done"], 1)
            nc.scalar.copy(xn_t[:].rearrange("p b t -> p (b t)"), ps_m[:]).then_inc(S["xnt_ready"], 1)
            act.wait_ge(S["q0_done"], 1)
            nc.scalar.copy(q_hi[:, 0, :], ps_m[:, 0:2 * P]).then_inc(S["hi_done"], 1)
            hi_count[0] = 1

            for s in range(SLOTS):
                n = s - 1
                if 0 <= n < HEADS:
                    act.wait_ge(S["negmax_ready"], n + 1)
                    for e in range(2):
                        nc.scalar.activation(prob[:, n % 2, 1024 * e:1024 * (e + 1)],
                                             ps_s[:, 1024 * e:1024 * (e + 1)], ACT.Exp,
                                             bias=neg_max[:, n:n + 1], accum_out=sums[:, n, e:e + 1])\
                            .then_inc(S["exp_done"], 1)
                for item in ring_items(s):
                    kind, n, g = item
                    i = RING[item]
                    if kind == "T":
                        act.wait_ge(S["ring_filled"], i + 1)
                        pp, row = part(n // 2, KPC * g)
                        nc.scalar.copy(pt_hi[:, pp, row:row + KPC, P * (n % 2):P * (n % 2 + 1)],
                                       ps_ring[:, i % 2, :].rearrange("p (k q) -> p k q", k=KPC))\
                            .then_inc(S["hi_done"], 1)
                    elif kind == "QO" and (s + 1) // 2 < PAIRS:
                        act.wait_ge(S["ring_filled"], i + 1)
                        nc.scalar.copy(q_hi[:, (s + 1) // 2 % 2, :], ps_ring[:, i % 2, 0:2 * P])\
                            .then_inc(S["hi_done"], 1)
                    if kind == "T" and g == 1:
                        for k, b in phases_at(s, 0):
                            rest(k, b)
                if not (0 <= s - 2 < HEADS):
                    for k, b in phases_at(s, 0):
                        rest(k, b)
                for k, b in phases_at(s, 1):
                    rest(k, b)

        @block.vector
        def _(dve):
            links = [0]
            his = [0]

            def link(ins):
                links[0] += 1
                ins.then_inc(S["dve_link"], 1)
                dve.wait_ge(S["dve_link"], links[0])

            def tt(o, a, b_, op):
                return nc.vector.tensor_tensor(o, a, b_, op)

            def statistics(src, eps, number, scale=None):
                link(nc.vector.bn_stats(st6[:, 0, :], src))
                link(nc.vector.bn_aggr(mv[:, 0, :], st6[:, 0, :]))
                nc.vector.tensor_scalar(var[:, 0:1], mv[:, 0, 1:2], scale or 1.0, eps, ALU.mult, ALU.add)\
                    .then_inc(S["var_ready"], 1)
                dve.wait_ge(S["rstd_ready"], number)

            def route(first, count):
                even = lid[:, 0:1, :].to_broadcast([P, count, LEAVES // 2])
                odd = lid[:, 1:2, :].to_broadcast([P, count, LEAVES // 2])
                link(nc.vector.tensor_copy(cur[:, 0:count, :], even))
                for level in range(DEPTH - 1, -1, -1):
                    n = 1 << level
                    w = (LEAVES // 2) // n
                    left = cur[:, 0:count, :].rearrange("p t (n w) -> p t n w", w=w)[:, :, :, 0]
                    if level == DEPTH - 1:
                        take = odd
                    else:
                        take = cur[:, 0:count, :].rearrange("p t (n w) -> p t n w", w=w)[:, :, :, w // 2]
                    link(nc.vector.copy_predicated(left, right[:, 0:count, n - 1:2 * n - 1], take))
                return nc.vector.tensor_copy(idx[:, first:first + count], cur[:, 0:count, 0])

            def hidden_layer(b, t):
                lf = leaf[t % 2]
                dve.wait_ge(S["prod_ready"], prods(b, t, 0))
                link(nc.vector.reduce_sum(hid[:], lf[:, 0:W1].rearrange("p (l d) -> p l d", l=LW), axis=AXX))
                if t < 3:
                    link(tt(hid[:], hid[:], lf[:, 2 * W1:2 * W1 + LW], ALU.add))
                    nc.vector.tensor_scalar_max(hid[:], hid[:], 0.0).then_inc(S["h_ready"], 1)
                else:
                    tt(hid[:], hid[:], lf[:, 2 * W1:2 * W1 + LW], ALU.add).then_inc(S["ff_pre"], 1)

            def leaf_output(b, t):
                lf = leaf[t % 2]
                dve.wait_ge(S["prod_ready"], prods(b, t, 1))
                link(nc.vector.reduce_sum(tree[:, t, :], lf[:, W1:2 * W1].rearrange("p (d l) -> p d l", l=LW),
                                          axis=AXX))
                tt(tree[:, t, :], tree[:, t, :], lf[:, 2 * W1 + LW:ROW], ALU.add).then_inc(S["leaf_taken"], 1)

            def groups(ap):
                return ap.rearrange("p (h v) -> p h v", h=RH)

            def rest(k, b):
                if k == 0:
                    dve.wait_ge(S["proj_done"], b + 1)
                    link(tt(x1[:], ps_m[:, 0:P], x_sb[:, b, :], ALU.add))
                    statistics(x1[:], EPS, pows(b, 0))
                    nc.vector.tensor_scalar(xn1[:], x1[:], mv[:, 0, 0:1], rstd[:, 0:1], ALU.subtract, ALU.mult)\
                        .then_inc(S["xn1_ready"], 1)
                elif k == 2:
                    dve.wait_ge(S["qk_done"], b + 1)
                    a = ps_m[:].rearrange("p (i n) -> p i n", i=4)
                    tt(qk_a[:], a[:, 0:2, :], xp[:, 0:2, :], ALU.mult).then_inc(S["dve_link"], 1)
                    links[0] += 1
                    link(tt(qk_b[:], a[:, 2:4, :], xp[:, 2:4, :], ALU.mult))
                    tt(qk_x[:], qk_a[:], qk_b[:], ALU.add).then_inc(S["qkx_ready"], 1)
                elif k == 3:
                    dve.wait_ge(S["eg_ready"], b + 1)
                    link(nc.vector.tensor_scalar_add(silu[:], silu[:], 1.0))
                    link(nc.vector.reciprocal(silu[:], silu[:]))
                    tt(silu[:], ps_m[:, P:2 * P], silu[:], ALU.mult).then_inc(S["silu_ready"], 1)
                elif k in (4, 5):
                    dve.wait_ge(S["sc_done"], 2 * b + k - 3)
                    hs = slice(4 * (k - 4), 4 * (k - 3))
                    tt(sm[:, hs, :], ps_m[:].rearrange("p (h n) -> p h n", h=4), dec[:, hs, :], ALU.mult)\
                        .then_inc(S["sm_ready"], 1)
                elif k == 6:
                    dve.wait_ge(S["y_done"], b + 1)
                    link(nc.vector.reduce_sum(gmean[:], groups(ps_m[:, 0:P]), axis=AXX))
                    link(nc.vector.tensor_scalar_mul(gmean[:], gmean[:], 1.0 / RE))
                    bc = gmean[:].rearrange("p (h o) -> p h o", o=1).to_broadcast([P, RH, RE])
                    link(tt(groups(yc), groups(ps_m[:, 0:P]), bc, ALU.subtract))
                    link(tt(ysq, yc, yc, ALU.mult))
                    link(nc.vector.reduce_sum(gmean[:], groups(ysq), axis=AXX))
                    nc.vector.tensor_scalar(var[:], gmean[:], 1.0 / RE, EPS, ALU.mult, ALU.add)\
                        .then_inc(S["var_ready"], 1)
                    dve.wait_ge(S["rstd_ready"], pows(b, 1))
                    bc = rstd[:].rearrange("p (h o) -> p h o", o=1).to_broadcast([P, RH, RE])
                    link(tt(groups(yc), groups(yc), bc, ALU.mult))
                    link(tt(yc, yc, gn[:, 0, :], ALU.mult))
                    link(tt(yc, yc, gn[:, 1, :], ALU.add))
                    tt(yc, yc, silu[:], ALU.mult).then_inc(S["gated_ready"], 1)
                elif k == 8:
                    dve.wait_ge(S["wo_done"], b + 1)
                    link(tt(x2[:], ps_m[:, 2 * P:3 * P], x1[:], ALU.add))
                    statistics(x2[:], EPS, pows(b, 2))
                    link(nc.vector.tensor_scalar(xl, x2[:], mv[:, 0, 0:1], rstd[:, 0:1], ALU.subtract, ALU.mult))
                    statistics(xl, 0.0, pows(b, 3), scale=D / (D - 1.0))
                    nc.vector.tensor_scalar(xf[:], xl, mv[:, 0, 0:1], rstd[:, 0:1], ALU.subtract, ALU.mult)\
                        .then_inc(S["xf_ready"], 1)
                elif k == 10:
                    dve.wait_ge(S["lg_done"], b + 1)
                    lg = ps_m[:].rearrange("p (t n) -> p t n", t=2)[:, :, 0:NODES]
                    nc.vector.scalar_tensor_tensor(right[:, 0:2, :], nb[:, 0:2, :], -1.0, lg, ALU.mult, ALU.is_lt)\
                        .then_inc(S["mask_ready"], 1)
                elif k == 11:
                    dve.wait_ge(S["lgv_done"], b + 1)
                    dve.wait_ge(S["mask_ready"], b + 1)
                    link(nc.vector.scalar_tensor_tensor(right[:, 2, :], nb[:, 2, :], -1.0, ps_m[:, 0:NODES],
                                                        ALU.mult, ALU.is_lt))
                    route(0, 3).then_inc(S["idx_ready"], 1)
                elif k == 12:
                    hidden_layer(b, 0)
                elif k == 13:
                    leaf_output(b, 0)
                    hidden_layer(b, 1)
                elif k == 14:
                    leaf_output(b, 1)
                    hidden_layer(b, 2)
                elif k == 15:
                    leaf_output(b, 2)
                elif k == 17:
                    dve.wait_ge(S["at_done"], b + 1)
                    link(nc.vector.reduce_max(att_nm[:], ps_m[:, 2 * P:3 * P], axis=AXX))
                    nc.vector.tensor_scalar_mul(att_nm[:], att_nm[:], -FSCALE).then_inc(S["nm_ready"], 1)
                elif k == 19:
                    dve.wait_ge(S["ap_ready"], b + 1)
                    link(nc.vector.reciprocal(att_r[:], att_sum[:]))
                    dve.wait_ge(S["yv_done"], b + 1)
                    nc.vector.scalar_tensor_tensor(y[:], ps_m[:, 0:P], att_r[:], xf[:], ALU.mult, ALU.add)\
                        .then_inc(S["y_ready"], 1)
                elif k == 21:
                    dve.wait_ge(S["lgf_done"], b + 1)
                    link(nc.vector.scalar_tensor_tensor(right[:, 0, :], nb[:, 3, :], -1.0,
                                                        ps_m[:, 256:256 + NODES], ALU.mult, ALU.is_lt))
                    route(3, 1).then_inc(S["idxf_ready"], 1)
                elif k == 22:
                    hidden_layer(b, 3)
                elif k == 23:
                    leaf_output(b, 3)
                    dve.wait_ge(S["leaf_taken"], 4 * b + 4)
                    link(tt(tree[:, 3, :], tree[:, 3, :], y[:], ALU.add))
                    if b >= 1:
                        dve.wait_ge(S["stored"], 16 * b)
                    tt(res[:], tree[:, 3, :], x2[:], ALU.add).then_inc(S["out_ready"], 1)

            dve.wait_ge(S["ld_x"], 16)
            for t in range(B):
                links[0] += 1
                nc.vector.bn_stats(st6[:, t, :], x_sb[:, t, :]).then_inc(S["dve_link"], 1)
            dve.wait_ge(S["dve_link"], links[0])
            for t in range(B):
                links[0] += 1
                nc.vector.bn_aggr(mv[:, t, :], st6[:, t, :]).then_inc(S["dve_link"], 1)
            dve.wait_ge(S["dve_link"], links[0])
            nc.vector.memset(var[:], 1.0).then_inc(S["dve_link"], 1)
            links[0] += 1
            dve.wait_ge(S["dve_link"], links[0])
            nc.vector.tensor_scalar_add(var[:, 0:B], mv[:, :, 1], EPS).then_inc(S["var_ready"], 1)
            dve.wait_ge(S["rstd_ready"], 1)
            for t in range(B):
                last = nc.vector.tensor_scalar(qmask[:, t, :], x_sb[:, t, :], mv[:, t, 0:1], rstd[:, t:t + 1],
                                               ALU.subtract, ALU.mult)
            last.then_inc(S["xn_ready"], 1)
            dve.wait_ge(S["wqk_done"], 1)
            nc.vector.tensor_scalar_mul(wqk[:].rearrange("p h d -> p (h d)")[:, 1024:2048], ps_s[:, 1024:2048], QSCALE)\
                .then_inc(S["wqk_b"], 1)
            dve.wait_ge(S["hi_done"], 1)
            tt(q_lo[:, 0, :], ps_m[:, 0:2 * P], q_hi[:, 0, :].bitcast(F32), ALU.subtract).then_inc(S["q0_ready"], 1)
            his[0] = 1

            def lower(n, g):
                i = RING[("T", n, g)]
                his[0] += 1
                dve.wait_ge(S["hi_done"], his[0])
                pp, row = part(n // 2, KPC * g)
                at = (slice(None), pp, slice(row, row + KPC), slice(P * (n % 2), P * (n % 2 + 1)))
                tt(pt_lo[at], ps_ring[:, i % 2, :].rearrange("p (k q) -> p k q", k=KPC), pt_hi[at].bitcast(F32),
                   ALU.subtract).then_inc(S["ring_free"], 1)

            def max_half(n, e):
                dve.wait_ge(S["s_done"], CH * n + 2 * e + 2)
                links[0] += 1
                nc.vector.reduce_max(chunk_max[:, n, e:e + 1], ps_s[:, 1024 * e:1024 * (e + 1)], axis=AXX)\
                    .then_inc(S["dve_link"], 1)

            for s in range(SLOTS):
                n, tr = s, s - 2
                taken = (s - 5) // 2
                if s % 2 and 0 <= taken < PAIRS:
                    dve.wait_ge(S["av_done"], 2 * taken + 2)
                    nc.vector.tensor_copy(av_sb[:], ps_av[:, 0:2 * P]).then_inc(S["av_taken"], 1)
                    two = slice(2 * taken, 2 * taken + 2)
                    link(nc.vector.reduce_sum(sum_all[:, two], sums[:, two, :], axis=AXX))
                    link(nc.vector.reciprocal(rsum[:, two], sum_all[:, two]))
                trs = 0 <= tr < HEADS
                if trs:
                    lower(tr, 0)
                if n < HEADS:
                    max_half(n, 0)
                if trs:
                    lower(tr, 1)
                for k, b in phases_at(s, 0):
                    rest(k, b)
                if n < HEADS:
                    max_half(n, 1)
                    dve.wait_ge(S["dve_link"], links[0])
                    nc.vector.tensor_reduce(neg_max[:, n:n + 1], chunk_max[:, n, :], axis=AXX, op=ALU.max,
                                            negate=True).then_inc(S["negmax_ready"], 1)
                if trs:
                    lower(tr, 2)
                    lower(tr, 3)
                if ("QO", s, 0) in RING:
                    i = RING[("QO", s, 0)]
                    dve.wait_ge(S["ring_filled"], i + 1)
                    last = None
                    if (s + 1) // 2 < PAIRS:
                        his[0] += 1
                        dve.wait_ge(S["hi_done"], his[0])
                        j = (s + 1) // 2 % 2
                        last = tt(q_lo[:, j, :], ps_ring[:, i % 2, 0:2 * P], q_hi[:, j, :].bitcast(F32), ALU.subtract)
                    if 0 <= taken < PAIRS:
                        two = slice(2 * taken, 2 * taken + 2)
                        bc = rsum[:, two].rearrange("p (h o) -> p h o", o=1).to_broadcast([P, 2, DH])
                        last = tt(o_sb[:], ps_ring[:, i % 2, 256:256 + P].rearrange("p (h e) -> p h e", h=2), bc,
                                  ALU.mult)
                    last.then_inc(S["ring_free"], 1)
                if ("OT", s, 0) in RING:
                    i = RING[("OT", s, 0)]
                    dve.wait_ge(S["ring_filled"], i + 1)
                    nc.vector.tensor_copy(ot_sb[:, (s - 6) // 2 % PPB, :], ps_ring[:, i % 2, 0:P])\
                        .then_inc(S["ring_free"], 1)
                for k, b in phases_at(s, 1):
                    rest(k, b)

        @block.gpsimd
        def _(pool):
            links = [0]

            def link(ins):
                links[0] += 1
                ins.then_inc(S["pool_link"], 1)
                pool.wait_ge(S["pool_link"], links[0])

            def power(n, count):
                pool.wait_ge(S["var_ready"], count)
                nc.gpsimd.tensor_tensor(rstd[:, 0:n], var[:, 0:n], half[:, 0, 0:n], ALU.pow).then_inc(S["rstd_ready"], 1)

            def split_ct(i):
                b, c = i // CH, i % CH
                pool.wait_ge(S[f"ld_ct{i % 2}"], 16 * (i // 2 + 1))
                if b:
                    pool.wait_ge(S["s_done"], CH * (H * b - 1) + c + 1)
                o = slice(512 * c, 512 * (c + 1))
                link(nc.gpsimd.tensor_copy(ct_hi[:, o], ct_stage[:, i % 2, :]))
                nc.gpsimd.tensor_tensor(ct_lo[:, o], ct_stage[:, i % 2, :], ct_hi[:, o].bitcast(F32), ALU.subtract)\
                    .then_inc(S["ct_split"], 1)

            def split_c(i):
                b, c = i // CH, i % CH
                pool.wait_ge(S[f"ld_c{i % 2}"], 16 * (i // 2 + 1))
                if b:
                    pool.wait_ge(S["av_done"], 2 * PPB * b - 1 + c // 2)
                o = slice(KPC * c, KPC * (c + 1))
                link(nc.gpsimd.tensor_copy(c_hi[:, o, :], c_stage[:, i % 2, :, :]))
                nc.gpsimd.tensor_tensor(c_lo[:, o, :], c_stage[:, i % 2, :, :], c_hi[:, o, :].bitcast(F32), ALU.subtract)\
                    .then_inc(S["c_split"], 1)

            def gather(b, t):
                nc.gpsimd.indirect_dma_start(
                    out=leaf[t % 2][:], out_offset=None, in_=leaves[t],
                    in_offset=bass.IndirectOffsetOnAxis(ap=idx[:, t:t + 1], axis=0),
                ).then_inc(S[f"gather{t % 2}"], 16)

            def up(b, t):
                lf = leaf[t % 2]
                src = (xf if t < 3 else y)[:].rearrange("p (o d) -> p o d", o=1).to_broadcast([P, LW, D])
                pool.wait_ge(S[f"gather{t % 2}"], 16 * (2 * b + t // 2 + 1))
                w = lf[:, 0:W1].rearrange("p (l d) -> p l d", l=LW)
                nc.gpsimd.tensor_tensor(w, w, src, ALU.mult).then_inc(S["prod_ready"], 1)

            def down(b, t):
                lf = leaf[t % 2]
                pool.wait_ge(S["h_ready"], 4 * b + t + 1)
                w = lf[:, W1:2 * W1].rearrange("p (d l) -> p d l", l=LW)
                h = hid[:].rearrange("p (o l) -> p o l", o=1).to_broadcast([P, D, LW])
                nc.gpsimd.tensor_tensor(w, w, h, ALU.mult).then_inc(S["prod_ready"], 1)

            def rest(k, b):
                if k == 0:
                    power(1, pows(b, 0))
                elif k == 2:
                    pool.wait_ge(S["qkx_ready"], b + 1)
                    q = qk_x[:, 0:1, :].to_broadcast([P, RH, P])
                    m = hmask[:].rearrange("p (h o) -> p h o", o=1).to_broadcast([P, RH, P])
                    nc.gpsimd.tensor_tensor(qmask[:], q, m, ALU.mult).then_inc(S["qmask_ready"], 1)
                elif k == 6:
                    power(RH, pows(b, 1))
                elif k == 8:
                    power(1, pows(b, 2))
                    pool.wait_ge(S["var_ready"], pows(b, 3))
                    link(nc.gpsimd.tensor_tensor(rstd[:, 1:2], var[:, 0:1], half[:, 1, 0:1], ALU.pow))
                    link(nc.gpsimd.tensor_scalar_add(rstd[:, 2:3], rstd[:, 1:2], EPS))
                    nc.gpsimd.tensor_tensor(rstd[:, 0:1], rstd[:, 2:3], half[:, 0, 0:1], ALU.pow)\
                        .then_inc(S["rstd_ready"], 1)
                elif k == 11:
                    pool.wait_ge(S["idx_ready"], b + 1)
                    if b >= 1:
                        pool.wait_ge(S["leaf_taken"], 4 * b)
                    gather(b, 0)
                    gather(b, 1)
                elif k == 12:
                    up(b, 0)
                    down(b, 0)
                    up(b, 1)
                elif k == 13:
                    pool.wait_ge(S["leaf_taken"], 4 * b + 1)
                    gather(b, 2)
                    down(b, 1)
                elif k == 14:
                    up(b, 2)
                    down(b, 2)
                elif k == 21:
                    pool.wait_ge(S["idxf_ready"], b + 1)
                    gather(b, 3)
                elif k == 22:
                    up(b, 3)
                    down(b, 3)

            nc.gpsimd.memset(half[:, 0, :], -0.5).then_inc(S["pool_link"], 1)
            link(nc.gpsimd.memset(half[:, 1, :], 0.5))
            links[0] += 1
            pool.wait_ge(S["pool_link"], links[0])
            power(B, 1)
            for c in range(CH):
                split_ct(c)
            for c in range(CH):
                split_c(c)
            pool.wait_ge(S["ld_rest"], 16 * 8)
            for s in range(SLOTS):
                for k, b in phases_at(s, 0):
                    rest(k, b)
                if s % H == H - 1 and s // H + 1 < B:
                    for c in range(CH):
                        split_ct(CH * (s // H + 1) + c)
                if s >= H and s % H == 1 and s // H < B:
                    split_c(CH * (s // H))
                    split_c(CH * (s // H) + 1)
                if s >= H and s % H == 2 and s // H < B:
                    split_c(CH * (s // H) + 2)
                    split_c(CH * (s // H) + 3)
                for k, b in phases_at(s, 1):
                    rest(k, b)


def _xpos_tables(np):
    f = np.float32
    half = RE // 2
    pos = np.arange(P, dtype=f)
    base = ((np.arange(0, RE, 2, dtype=f) + f(0.4 * RE)) / f(1.4 * RE)).astype(f)
    scale = (base[None, :] ** (pos[:, None] / f(512.0))).astype(f)
    inv_freq = (f(1.0) / f(10000.0) ** (np.arange(half, dtype=f) / f(half))).astype(f)
    ang = (pos[:, None] * inv_freq[None, :]).astype(f)
    sin, cos = np.sin(ang), np.cos(ang)
    sign = np.tile(np.array([-1.0, 1.0], f), half)
    out = []
    for trig, sg in ((cos, None), (sin, sign)):
        for sc in (scale, (f(1.0) / scale).astype(f)):
            t = np.repeat((trig * sc).astype(f), 2, axis=-1)
            t = t if sg is None else t * sg[None, :]
            out.append(np.tile(t.T, (RH, 1)))
    return np.ascontiguousarray(np.stack(out, 1).astype(f))


def _decay(np):
    f = np.float32
    lo, hi = np.log(1.0 / 32.0), np.log(1.0 / 512.0)
    gam = (f(1.0) - np.exp(np.linspace(lo, hi, RH).astype(f)).astype(f)).astype(f)
    n, m = np.arange(P)[None, :], np.arange(P)[:, None]
    e = (n - m).astype(f)[None] * np.log(gam).astype(f)[:, None, None]
    d = np.where((n >= m)[None], np.exp(np.minimum(e, 0)), 0.0).astype(f)
    return np.ascontiguousarray(d.transpose(1, 0, 2))


def kernel(**inputs):
    import numpy as np
    import concourse.bacc as bacc
    from concourse import mybir as mb
    from concourse.bass_utils import run_bass_kernel_spmd as run

    g = {k: np.asarray(v) for k, v in inputs.items()}
    heads = lambda w: w.transpose(1, 0, 2).reshape(D, RH * RE)
    swap = np.arange(D) ^ 1
    wq, wk, wv = (heads(g[f"L0_attn_W_{c}"]) for c in "QKV")
    small = np.stack([wq, wk, wq[:, swap], wk[:, swap], wv, g["L0_attn_W_G"], g["L0_attn_W_O"]], 1)
    trees = "qkvf"

    def rows(t):
        w1 = g[f"L0_ffn_{t}_w1"].transpose(0, 2, 1).reshape(LEAVES, W1)
        w2 = g[f"L0_ffn_{t}_w2"].transpose(0, 2, 1).reshape(LEAVES, W1)
        return np.concatenate([w1, w2, g[f"L0_ffn_{t}_b1"], g[f"L0_ffn_{t}_b2"]], 1)

    ids = np.arange(LEAVES, dtype=np.float32)
    arrays = {
        "x": g["x"],
        "ctx_rows": g["ctx_1024"],
        "ctx_t": g["ctx_1024"].transpose(0, 2, 1),
        "wq_t": g["L0_xattn_w_q"].T,
        "wk_t": g["L0_xattn_w_k"].T,
        "w_v": g["L0_xattn_w_v"],
        "w_o": g["L0_xattn_w_o"],
        "w_small": small,
        "xpos": _xpos_tables(np),
        "decay": _decay(np),
        "head_mask": (np.arange(P)[:, None] // RE == np.arange(RH)[None, :]).astype(np.float32),
        "gn_wb": np.stack([g["L0_attn_gn_weight"], g["L0_attn_gn_bias"]], 0),
        "node_w": np.stack([g[f"L0_ffn_{t}_nw"].T for t in trees], 1),
        "node_b": np.stack([g[f"L0_ffn_{t}_nb"] for t in trees], 0),
        **{f"leaves_{t}": rows(t) for t in trees},
        "leaf_ids": np.stack([ids[0::2], ids[1::2]], 0),
        "ident_in": np.eye(P, dtype=np.float32),
    }
    arrays = {f"{k}_dram": np.ascontiguousarray(v) for k, v in arrays.items()}
    nc = bacc.Bacc("TRN2", target_bir_lowering=False, num_devices=1)
    ap = {k[:-5]: nc.dram_tensor(k, v.shape, mb.dt.from_np(v.dtype), kind="ExternalInput").ap()
          for k, v in arrays.items()}
    out = nc.dram_tensor("out_dram", (B, P, D), mb.dt.float32, kind="ExternalOutput").ap()
    leaves = [ap.pop(f"leaves_{t}") for t in trees]
    program(nc, leaves=leaves, out=out, **ap)
    r = run(nc, [arrays], core_ids=[0])
    return r.results[0]["out_dram"]
```

```python
import concourse.bass as bass
from concourse import mybir
from contextlib import ExitStack

F32 = mybir.dt.float32
F32R = mybir.dt.float32r
I32 = mybir.dt.int32
ALU = mybir.AluOpType
ACT = mybir.ActivationFunctionType
AXX = mybir.AxisListType.X

P = 128
D = 128
B = 4
NK = 2048
H, DH = 16, 64
HEADS = B * H
PAIRS = HEADS // 2
PPB = H // 2
KT = NK // P
CH = 4
KPC = KT // CH
RH, RE = 8, 16
LEAVES, NODES, DEPTH, LW = 256, 255, 8, 16
W1 = D * LW
ROW = 2 * W1 + LW + D
EPS = 1e-5
QSCALE = DH ** -0.5
FSCALE = D ** -0.5

PE_AT = dict(proj=43, xn1_t=44, qk=45, vg=46, score0=47, score1=48, yv=49, gated_t=51, wo=52, xf_t=54,
             logits=55, logits_v=56, qk_t=67, att=68, attp_t=69, attv=70, y_t=71, logits_f=72)
ACT_AT = dict(xn1_t=44, vg=46, gated_t=51, xf_t=54, qk_t=67, att=68, attp_t=69, y_t=71, gelu=76)
DVE_AT = dict(x1=43, rope=45, silu=46, decay0=47, decay1=48, norm=49, x2=53, turns=55, route=56,
              hid0=60, hid1=61, out0=62, out1=63, hid2=64, out2=66, attmax=68, y=70, route_f=72,
              hid3=76, out3=78)
POOL_AT = dict(root1=43, mask_q=45, root_n=49, roots2=53, gather01=57, up0=59, up1=60, down0=61,
               down1=62, gather2=63, up2=64, down2=65, gather3=73, up3=75, down3=77)
LAST = max(max(t.values()) for t in (PE_AT, ACT_AT, DVE_AT, POOL_AT))
SLOTS = H * (B - 1) + LAST // 2 + 1


def steps_at(table, slot, place):
    return [(k, b) for b in range(B) for k, u in table.items() if 2 * H * b + u == 2 * slot + place]


def query_pair(slot):
    return (slot + 2) // 2 if slot % 2 == 0 and (slot + 2) // 2 < PAIRS else None


def ot_pair(slot):
    return (slot - 6) // 2 if slot % 2 == 0 and 0 <= (slot - 6) // 2 < PAIRS else None


def o_pair(slot):
    return (slot - 5) // 2 if slot % 2 and 0 <= (slot - 5) // 2 < PAIRS else None


def ring_items(slot):
    out = [("T", slot - 2, g) for g in range(CH)] if 0 <= slot - 2 < HEADS else []
    if query_pair(slot) is not None or ot_pair(slot) is not None or o_pair(slot) is not None:
        out.append(("X", slot, 0))
    return out


RING, BY_DVE, BY_ACT = {}, {}, {}
for _slot in range(SLOTS):
    for _item in ring_items(_slot):
        RING[_item] = len(RING)
        if _item[0] == "T" or query_pair(_slot) is not None:
            BY_DVE[_item] = len(BY_DVE) + 1
        if _item[0] == "X" and (ot_pair(_slot) is not None or o_pair(_slot) is not None):
            BY_ACT[_item] = len(BY_ACT) + 1
RING_ORDER = list(RING)


def program(nc, x, ctx_rows, ctx_t, wq_t, wk_t, w_v, w_o, w_small, xpos, decay, head_mask, gn_wb, node_w,
            node_b, leaves, leaf_ids, ident_in, out):
    es = ExitStack()
    with es:
        def sb(name, shape, dt=F32):
            return es.enter_context(nc.sbuf_tensor(name, shape, dt))

        def pb(name, shape):
            return es.enter_context(nc.psum_tensor(name, shape, F32))

        def sem(name):
            return es.enter_context(nc.semaphore(name))

        ct_stage = sb("ct_stage", [P, 2, 512])
        c_stage = sb("c_stage", [P, 2, KPC, D])
        ct_hi, ct_lo = sb("ct_hi", [P, NK], F32R), sb("ct_lo", [P, NK], F32R)
        c_hi, c_lo = sb("c_hi", [P, KT, D], F32R), sb("c_lo", [P, KT, D], F32R)
        prob = sb("prob", [P, 2, NK])
        pt_hi = sb("pt_hi", [P, 3, KT // 2, 2 * P], F32R)
        pt_lo = sb("pt_lo", [P, 3, KT // 2, 2 * P], F32R)
        q_hi, q_lo = sb("q_hi", [P, 2, 2 * P], F32R), sb("q_lo", [P, 2, 2 * P], F32R)
        wqk = sb("wqk", [P, H, D])
        wv = sb("wv", [P, H * DH])
        wo = sb("wo", [P, PPB, D])
        x_sb = sb("x_sb", [P, B, D])
        xn_t = sb("xn_t", [P, B, P])
        av_sb = sb("av_sb", [P, 2 * P])
        o_sb = sb("o_sb", [P, 2, DH])
        ot_sb = sb("ot_sb", [P, PPB, P])
        chunk_max = sb("chunk_max", [P, HEADS, 2])
        neg_max = sb("neg_max", [P, HEADS])
        sums = sb("sums", [P, HEADS, 2])
        sum_all = sb("sum_all", [P, HEADS])
        rsum = sb("rsum", [P, HEADS])
        ident = sb("ident", [P, P])
        wsm = sb("wsm", [P, 7, D])
        xp = sb("xp", [P, 4, P])
        dec = sb("dec", [P, RH, P])
        hmask = sb("hmask", [P, RH])
        gn = sb("gn", [P, 2, D])
        nw = sb("nw", [P, 4, NODES])
        nb = sb("nb", [P, 4, NODES])
        lid = sb("lid", [P, 2, LEAVES // 2])
        st6 = sb("st6", [P, B, 6])
        mv = sb("mv", [P, B, 2])
        var = sb("var", [P, RH])
        rstd = sb("rstd", [P, RH])
        half = sb("half", [P, 2, RH])
        x1, x2, xf, y = sb("x1", [P, D]), sb("x2", [P, D]), sb("xf", [P, D]), sb("y", [P, D])
        xn1, tr_sb = sb("xn1", [P, D]), sb("tr_sb", [P, 2, P])
        qk_a, qk_b, qk_x = sb("qk_a", [P, 2, P]), sb("qk_b", [P, 2, P]), sb("qk_x", [P, 2, P])
        xl = qk_b[:, 0, :]
        v_sb, silu = sb("v_sb", [P, D]), sb("silu", [P, D])
        qmask = sb("qmask", [P, RH, P])
        sm = qmask
        gmean = sb("gmean", [P, RH])
        yc, ysq = qk_a[:, 0, :], qk_a[:, 1, :]
        right = sb("right", [P, 3, NODES], I32)
        cur = sb("cur", [P, 3, LEAVES // 2])
        idx = sb("idx", [P, 4], I32)
        leaf = [sb("leaf0", [P, ROW]), sb("leaf1", [P, ROW])]
        hid = sb("hid", [P, 4, LW])
        tree = sb("tree", [P, 4, D])
        att_nm, att_sum, att_r = sb("att_nm", [P, 1]), sb("att_sum", [P, 1]), sb("att_r", [P, 1])
        att_p = xn1
        res = sb("res", [P, D])

        ps_s = pb("ps_s", [P, NK])
        ps_ring = pb("ps_ring", [P, 2, 512])
        ps_av = pb("ps_av", [P, 512])
        ps_m = pb("ps_m", [P, 512])

        names = """ld_x ld_wqk ld_ct0 ld_ct1 ld_c0 ld_c1 ld_wvo ld_rest gather0 gather1 stored
            var_ready rstd_ready xn_ready xnt_done xnt_ready wqk_done wqk_a wqk_b q0_done q0_ready
            ct_split c_split s_done negmax_ready exp_done ring_filled ring_free ring_taken hi_done av_done av_taken
            dve_link pool_link proj_done xn1_ready xn1t_done tr_ready qk_done qkx_ready qmask_ready vg_done
            v_ready eg_ready silu_ready rsum_ready sc_done sm_ready y_done gated_ready gatedt_done wo_done xf_ready
            xft_done lg_done mask_ready lgv_done idx_ready prod_ready h_ready leaf_taken ff_pre
            qkt_done at_done nm_ready ap_ready apt_done yv_done y_ready yt_done lgf_done idxf_ready
            out_ready""".split()
        S = {n: sem(n) for n in names}
        block = es.enter_context(nc.Block())

        def part(pair, kt):
            return (0, kt) if kt < KT // 2 else (1 + pair % 2, kt - KT // 2)

        def wqk_at(h):
            return (h % 2) * (H // 2) + h // 2

        def pows(b, i):
            return 2 + 4 * b + i

        products = sorted((POOL_AT[f"{k}{t}"], t, i) for t in range(4) for i, k in enumerate(("up", "down")))

        def prods(b, tree_no, step):
            return 8 * b + [p[1:] for p in products].index((tree_no, step)) + 1

        def store(sp, b):
            sp.wait_ge(S["out_ready"], b + 1)
            sp.dma_start(out[b], res[:]).then_inc(S["stored"], 16)

        @block.sync
        def _(sp):
            def load_ct(i):
                if i >= 2:
                    sp.wait_ge(S["ct_split"], i - 1)
                sp.dma_start(ct_stage[:, i % 2, :], ctx_t[i // CH, :, 512 * (i % CH):512 * (i % CH + 1)])\
                    .then_inc(S[f"ld_ct{i % 2}"], 16)

            def load_c(i):
                if i >= 2:
                    sp.wait_ge(S["c_split"], i - 1)
                rows = ctx_rows[i // CH, 512 * (i % CH):512 * (i % CH + 1), :]
                sp.dma_start(c_stage[:, i % 2, :, :], rows.rearrange("(k p) d -> p k d", p=P))\
                    .then_inc(S[f"ld_c{i % 2}"], 16)

            sp.dma_start(x_sb[:], x.rearrange("b p d -> p b d")).then_inc(S["ld_x"], 16)
            load_ct(0)
            load_ct(1)
            sp.dma_start(wv[:], w_v).then_inc(S["ld_wvo"], 16)
            sp.dma_start(wo[:], w_o.rearrange("(i p) n -> p i n", p=P)).then_inc(S["ld_wvo"], 16)
            load_ct(2)
            load_ct(3)
            load_c(0)
            load_c(1)
            sp.dma_start(wsm[:], w_small).then_inc(S["ld_rest"], 16)
            sp.dma_start(xp[:], xpos).then_inc(S["ld_rest"], 16)
            sp.dma_start(dec[:], decay).then_inc(S["ld_rest"], 16)
            sp.dma_start(hmask[:], head_mask).then_inc(S["ld_rest"], 16)
            sp.dma_start(gn[:], gn_wb.partition_broadcast(P)).then_inc(S["ld_rest"], 16)
            sp.dma_start(nw[:], node_w).then_inc(S["ld_rest"], 16)
            sp.dma_start(nb[:], node_b.partition_broadcast(P)).then_inc(S["ld_rest"], 16)
            sp.dma_start(lid[:], leaf_ids.partition_broadcast(P)).then_inc(S["ld_rest"], 16)
            load_c(2)
            load_c(3)
            for b in range(B):
                if b + 1 < B:
                    for c in range(CH):
                        load_ct(CH * (b + 1) + c)
                    for c in range(CH):
                        load_c(CH * (b + 1) + c)
                if b >= 1:
                    store(sp, b - 1)
            store(sp, B - 1)
            sp.wait_ge(S["stored"], 16 * B)

        @block.tensor
        def _(pe):
            def mm(o, l, r, start=True, stop=True):
                return nc.tensor.matmul(o, l, r, start=start, stop=stop)

            def ring_slot(item):
                i = RING[item]
                if i >= 2:
                    before = RING_ORDER[i - 2]
                    if before in BY_DVE:
                        pe.wait_ge(S["ring_free"], BY_DVE[before])
                    if before in BY_ACT:
                        pe.wait_ge(S["ring_taken"], BY_ACT[before])
                return ps_ring[:, i % 2, :]

            def rest(k, b):
                if k == "proj":
                    pe.wait_ge(S["ring_taken"], BY_ACT[("X", H * b + 2 * (PPB - 1) + 6, 0)])
                    if b >= 1:
                        pe.wait_ge(S["idxf_ready"], b)
                    for i in range(PPB):
                        last = mm(ps_m[:, 0:P], ot_sb[:, i, :], wo[:, i, :], i == 0, i == PPB - 1)
                    last.then_inc(S["proj_done"], 1)
                elif k == "xn1_t":
                    pe.wait_ge(S["xn1_ready"], b + 1)
                    nc.tensor.transpose(ps_m[:, P:2 * P], xn1[:], ident[:]).then_inc(S["xn1t_done"], 1)
                elif k == "qk":
                    pe.wait_ge(S["tr_ready"], 6 * b + 1)
                    for i in range(4):
                        last = mm(ps_m[:, i * P:(i + 1) * P], wsm[:, i, :], tr_sb[:, 0, :])
                    last.then_inc(S["qk_done"], 1)
                elif k == "vg":
                    pe.wait_ge(S["qkx_ready"], b + 1)
                    mm(ps_m[:, 0:P], tr_sb[:, 0, :], wsm[:, 4, :])
                    mm(ps_m[:, P:2 * P], tr_sb[:, 0, :], wsm[:, 5, :]).then_inc(S["vg_done"], 1)
                elif k in ("score0", "score1"):
                    first = 4 * (k == "score1")
                    if not first:
                        pe.wait_ge(S["qmask_ready"], b + 1)
                        pe.wait_ge(S["v_ready"], b + 1)
                        pe.wait_ge(S["silu_ready"], b + 1)
                    else:
                        pe.wait_ge(S["sm_ready"], 2 * b + 1)
                    mm(ps_m[:], qk_x[:, 1, :], qmask[:, first:first + 4, :]).then_inc(S["sc_done"], 1)
                elif k == "yv":
                    pe.wait_ge(S["sm_ready"], 2 * b + 2)
                    for h in range(RH):
                        last = mm(ps_m[:, RE * h:RE * (h + 1)], sm[:, h, :], v_sb[:, RE * h:RE * (h + 1)])
                    last.then_inc(S["y_done"], 1)
                elif k == "gated_t":
                    pe.wait_ge(S["gated_ready"], b + 1)
                    nc.tensor.transpose(ps_m[:, P:2 * P], yc, ident[:]).then_inc(S["gatedt_done"], 1)
                elif k == "wo":
                    pe.wait_ge(S["tr_ready"], 6 * b + 2)
                    mm(ps_m[:, 2 * P:3 * P], tr_sb[:, 1, :], wsm[:, 6, :]).then_inc(S["wo_done"], 1)
                elif k == "xf_t":
                    pe.wait_ge(S["xf_ready"], b + 1)
                    nc.tensor.transpose(ps_m[:, 0:P], xf[:], ident[:]).then_inc(S["xft_done"], 1)
                elif k == "logits":
                    pe.wait_ge(S["tr_ready"], 6 * b + 3)
                    mm(ps_m[:, 0:NODES], tr_sb[:, 0, :], nw[:, 0, :])
                    mm(ps_m[:, 256:256 + NODES], tr_sb[:, 0, :], nw[:, 1, :]).then_inc(S["lg_done"], 1)
                elif k == "logits_v":
                    pe.wait_ge(S["mask_ready"], b + 1)
                    mm(ps_m[:, 0:NODES], tr_sb[:, 0, :], nw[:, 2, :]).then_inc(S["lgv_done"], 1)
                elif k == "qk_t":
                    pe.wait_ge(S["leaf_taken"], 4 * b + 3)
                    nc.tensor.transpose(ps_m[:, 0:P], tree[:, 0, :], ident[:])
                    nc.tensor.transpose(ps_m[:, P:2 * P], tree[:, 1, :], ident[:]).then_inc(S["qkt_done"], 1)
                elif k == "att":
                    pe.wait_ge(S["tr_ready"], 6 * b + 4)
                    mm(ps_m[:, 2 * P:3 * P], tr_sb[:, 0, :], tr_sb[:, 1, :]).then_inc(S["at_done"], 1)
                elif k == "attp_t":
                    pe.wait_ge(S["ap_ready"], b + 1)
                    nc.tensor.transpose(ps_m[:, 3 * P:4 * P], att_p[:], ident[:]).then_inc(S["apt_done"], 1)
                elif k == "attv":
                    pe.wait_ge(S["tr_ready"], 6 * b + 5)
                    mm(ps_m[:, 0:P], tr_sb[:, 0, :], tree[:, 2, :]).then_inc(S["yv_done"], 1)
                elif k == "y_t":
                    pe.wait_ge(S["y_ready"], b + 1)
                    nc.tensor.transpose(ps_m[:, P:2 * P], y[:], ident[:]).then_inc(S["yt_done"], 1)
                elif k == "logits_f":
                    pe.wait_ge(S["tr_ready"], 6 * b + 6)
                    mm(ps_m[:, 256:256 + NODES], tr_sb[:, 1, :], nw[:, 3, :]).then_inc(S["lgf_done"], 1)

            def scores(n, c):
                b, h = n // H, n % H
                if h == 0:
                    pe.wait_ge(S["ct_split"], CH * b + c + 1)
                if n == 0 and c == 0:
                    pe.wait_ge(S["q0_ready"], 1)
                elif n % 2 == 0 and c == 0:
                    pe.wait_ge(S["ring_free"], BY_DVE[("X", n - 2, 0)])
                if n >= 1 and c % 2 == 0:
                    pe.wait_ge(S["exp_done"], 2 * (n - 1) + c // 2 + 1)
                o = ps_s[:, 512 * c:512 * (c + 1)]
                j = (n // 2) % 2
                qh, ql = q_hi[:, j, P * (n % 2):P * (n % 2 + 1)], q_lo[:, j, P * (n % 2):P * (n % 2 + 1)]
                kh, kl = ct_hi[:, 512 * c:512 * (c + 1)], ct_lo[:, 512 * c:512 * (c + 1)]
                mm(o, qh, kh, True, False)
                mm(o, qh, kl, False, False)
                mm(o, ql, kh, False, True).then_inc(S["s_done"], 1)

            def transposes(n, g):
                pe.wait_ge(S["exp_done"], 2 * n + g // 2 + 1)
                o = ring_slot(("T", n, g))
                for i in range(KPC):
                    k = (KPC * g + i) * P
                    last = nc.tensor.transpose(o[:, i * P:(i + 1) * P], prob[:, n % 2, k:k + P], ident[:])
                last.then_inc(S["ring_filled"], 1)

            def context_half(pair, half_no):
                b = pair // PPB
                pe.wait_ge(S["ring_free"], BY_DVE[("T", 2 * pair + 1, 2 * half_no + 1)])
                if pair % PPB == 0:
                    pe.wait_ge(S["c_split"], CH * b + 2 * (half_no + 1))
                if half_no == 0 and pair >= 1:
                    pe.wait_ge(S["av_taken"], pair)
                for kt in range(8 * half_no, 8 * half_no + 8):
                    pp, row = part(pair, kt)
                    first, end = kt == 0, kt == KT - 1
                    mm(ps_av[:, 0:2 * P], c_hi[:, kt, :], pt_hi[:, pp, row, :], first, False)
                    mm(ps_av[:, 0:2 * P], c_hi[:, kt, :], pt_lo[:, pp, row, :], False, False)
                    last = mm(ps_av[:, 0:2 * P], c_lo[:, kt, :], pt_hi[:, pp, row, :], False, end)
                last.then_inc(S["av_done"], 1)

            def queries(pair, o):
                for j in range(2):
                    last = mm(o[:, j * P:(j + 1) * P], wqk[:, wqk_at((2 * pair + j) % H), :], xn_t[:, pair // PPB, :])
                return last

            pe.wait_ge(S["ld_wqk"], 48)
            for h in range(H):
                r, at = DH * (h % 2), wqk_at(h)
                last = mm(ps_s[:, at * D:(at + 1) * D], prob[r:r + DH, 0, (h // 2) * D:(h // 2 + 1) * D],
                          prob[r:r + DH, 1, (h // 2) * D:(h // 2 + 1) * D])
            last.then_inc(S["wqk_done"], 1)
            pe.wait_ge(S["xn_ready"], 1)
            for t in range(B):
                last = nc.tensor.transpose(ps_m[:, t * P:(t + 1) * P], qmask[:, t, :], ident[:])
            last.then_inc(S["xnt_done"], 1)
            pe.wait_ge(S["wqk_a"], 1)
            pe.wait_ge(S["wqk_b"], 1)
            pe.wait_ge(S["xnt_ready"], 1)
            queries(0, ps_m).then_inc(S["q0_done"], 1)

            for s in range(SLOTS):
                head = s if s < HEADS else None
                tr = s - 2 if 0 <= s - 2 < HEADS else None
                for c in range(CH):
                    if tr is not None and c < 2:
                        transposes(tr, c)
                    if head is not None:
                        scores(head, c)
                    if c == 1:
                        for k, b in steps_at(PE_AT, s, 0):
                            rest(k, b)
                    if tr is not None and c >= 2:
                        transposes(tr, c)
                for k, b in steps_at(PE_AT, s, 1):
                    rest(k, b)
                if s % 2 and 0 <= (s - 3) // 2 < PAIRS:
                    context_half((s - 3) // 2, 0)
                if s % 2 == 0 and 0 <= (s - 4) // 2 < PAIRS:
                    context_half((s - 4) // 2, 1)
                if ("X", s, 0) in RING:
                    o = ring_slot(("X", s, 0))
                    if query_pair(s) is not None:
                        last = queries(query_pair(s), o)
                    if ot_pair(s) is not None:
                        pe.wait_ge(S["ring_taken"], BY_ACT[("X", s - 1, 0)])
                        last = nc.tensor.transpose(o[:, 256:256 + P], o_sb[:].rearrange("p a b -> p (a b)"), ident[:])
                    if o_pair(s) is not None:
                        pair = o_pair(s)
                        if pair == 0:
                            pe.wait_ge(S["ld_wvo"], 32)
                        pe.wait_ge(S["av_taken"], pair + 1)
                        for j in range(2):
                            h = (2 * pair + j) % H
                            last = mm(o[:, DH * j:DH * (j + 1)], av_sb[:, j * P:(j + 1) * P], wv[:, DH * h:DH * (h + 1)])
                    last.then_inc(S["ring_filled"], 1)

        @block.scalar
        def _(act):
            hi_count = [0]

            def rest(k, b):
                if k == "xn1_t":
                    act.wait_ge(S["xn1t_done"], b + 1)
                    nc.scalar.copy(tr_sb[:, 0, :], ps_m[:, P:2 * P]).then_inc(S["tr_ready"], 1)
                elif k == "vg":
                    act.wait_ge(S["vg_done"], b + 1)
                    nc.scalar.copy(v_sb[:], ps_m[:, 0:P]).then_inc(S["v_ready"], 1)
                    nc.scalar.activation(silu[:], ps_m[:, P:2 * P], ACT.Exp, scale=-1.0).then_inc(S["eg_ready"], 1)
                elif k == "gated_t":
                    act.wait_ge(S["gatedt_done"], b + 1)
                    nc.scalar.copy(tr_sb[:, 1, :], ps_m[:, P:2 * P]).then_inc(S["tr_ready"], 1)
                elif k == "xf_t":
                    act.wait_ge(S["xft_done"], b + 1)
                    nc.scalar.copy(tr_sb[:, 0, :], ps_m[:, 0:P]).then_inc(S["tr_ready"], 1)
                elif k == "qk_t":
                    act.wait_ge(S["qkt_done"], b + 1)
                    nc.scalar.copy(tr_sb[:].rearrange("p a b -> p (a b)"), ps_m[:, 0:2 * P])\
                        .then_inc(S["tr_ready"], 1)
                elif k == "att":
                    act.wait_ge(S["nm_ready"], b + 1)
                    nc.scalar.activation(att_p[:], ps_m[:, 2 * P:3 * P], ACT.Exp, bias=att_nm[:], scale=FSCALE,
                                         accum_out=att_sum[:]).then_inc(S["ap_ready"], 1)
                elif k == "attp_t":
                    act.wait_ge(S["apt_done"], b + 1)
                    nc.scalar.copy(tr_sb[:, 0, :], ps_m[:, 3 * P:4 * P]).then_inc(S["tr_ready"], 1)
                elif k == "y_t":
                    act.wait_ge(S["yt_done"], b + 1)
                    nc.scalar.copy(tr_sb[:, 1, :], ps_m[:, P:2 * P]).then_inc(S["tr_ready"], 1)
                elif k == "gelu":
                    act.wait_ge(S["ff_pre"], b + 1)
                    nc.scalar.activation(hid[:, 3, :], hid[:, 3, :], ACT.Gelu).then_inc(S["h_ready"], 1)

            act.dma_start(ident[:], ident_in).then_inc(S["ld_wqk"], 16)
            act.dma_start(prob[:, 0, 0:PPB * D].rearrange("p (i d) -> p i d", i=PPB),
                          wq_t.rearrange("(i p) d -> p i d", p=P)).then_inc(S["ld_wqk"], 16)
            act.dma_start(prob[:, 1, 0:PPB * D].rearrange("p (i d) -> p i d", i=PPB),
                          wk_t.rearrange("(i p) d -> p i d", p=P)).then_inc(S["ld_wqk"], 16)
            wqk_flat = wqk[:].rearrange("p h d -> p (h d)")
            act.wait_ge(S["wqk_done"], 1)
            nc.scalar.activation(wqk_flat[:, 0:1024], ps_s[:, 0:1024], ACT.Copy, scale=QSCALE)\
                .then_inc(S["wqk_a"], 1)
            act.wait_ge(S["xnt_done"], 1)
            nc.scalar.copy(xn_t[:].rearrange("p b t -> p (b t)"), ps_m[:]).then_inc(S["xnt_ready"], 1)
            act.wait_ge(S["q0_done"], 1)
            nc.scalar.copy(q_hi[:, 0, :], ps_m[:, 0:2 * P]).then_inc(S["hi_done"], 1)
            hi_count[0] = 1

            for s in range(SLOTS):
                n = s - 1
                if 0 <= n < HEADS:
                    act.wait_ge(S["negmax_ready"], n + 1)
                    for e in range(2):
                        nc.scalar.activation(prob[:, n % 2, 1024 * e:1024 * (e + 1)],
                                             ps_s[:, 1024 * e:1024 * (e + 1)], ACT.Exp,
                                             bias=neg_max[:, n:n + 1], accum_out=sums[:, n, e:e + 1])\
                            .then_inc(S["exp_done"], 1)
                if ("X", s - 1, 0) in RING:
                    i = RING[("X", s - 1, 0)]
                    act.wait_ge(S["ring_filled"], i + 1)
                    if ot_pair(s - 1) is not None:
                        nc.scalar.copy(ot_sb[:, ot_pair(s - 1) % PPB, :], ps_ring[:, i % 2, 256:256 + P])\
                            .then_inc(S["ring_taken"], 1)
                    if query_pair(s - 1) is not None:
                        nc.scalar.copy(q_hi[:, query_pair(s - 1) % 2, :], ps_ring[:, i % 2, 0:2 * P])\
                            .then_inc(S["hi_done"], 1)
                    if o_pair(s - 1) is not None:
                        pair = o_pair(s - 1)
                        act.wait_ge(S["rsum_ready"], pair + 1)
                        for j in range(2):
                            last = nc.scalar.activation(o_sb[:, j, :], ps_ring[:, i % 2, DH * j:DH * (j + 1)], ACT.Copy,
                                                        scale=rsum[:, 2 * pair + j:2 * pair + j + 1])
                        last.then_inc(S["ring_taken"], 1)
                taken = (s - 5) // 2
                if s % 2 and 0 <= taken < PAIRS:
                    act.wait_ge(S["av_done"], 2 * taken + 2)
                    nc.scalar.copy(av_sb[:], ps_av[:, 0:2 * P]).then_inc(S["av_taken"], 1)
                for g in range(CH):
                    n = s - 2
                    if 0 <= n < HEADS:
                        i = RING[("T", n, g)]
                        act.wait_ge(S["ring_filled"], i + 1)
                        pp, row = part(n // 2, KPC * g)
                        nc.scalar.copy(pt_hi[:, pp, row:row + KPC, P * (n % 2):P * (n % 2 + 1)],
                                       ps_ring[:, i % 2, :].rearrange("p (k q) -> p k q", k=KPC))\
                            .then_inc(S["hi_done"], 1)
                    if g == 1:
                        for k, b in steps_at(ACT_AT, s, 0):
                            rest(k, b)
                for k, b in steps_at(ACT_AT, s, 1):
                    rest(k, b)

        @block.vector
        def _(dve):
            links = [0]
            his = [0]

            def link(ins):
                links[0] += 1
                ins.then_inc(S["dve_link"], 1)
                dve.wait_ge(S["dve_link"], links[0])

            def tt(o, a, b_, op):
                return nc.vector.tensor_tensor(o, a, b_, op)

            def statistics(src, eps, number, scale=None):
                link(nc.vector.bn_stats(st6[:, 0, :], src))
                link(nc.vector.bn_aggr(mv[:, 0, :], st6[:, 0, :]))
                nc.vector.tensor_scalar(var[:, 0:1], mv[:, 0, 1:2], scale or 1.0, eps, ALU.mult, ALU.add)\
                    .then_inc(S["var_ready"], 1)
                dve.wait_ge(S["rstd_ready"], number)

            def route(first, count):
                even = lid[:, 0:1, :].to_broadcast([P, count, LEAVES // 2])
                odd = lid[:, 1:2, :].to_broadcast([P, count, LEAVES // 2])
                link(nc.vector.tensor_copy(cur[:, 0:count, :], even))
                for level in range(DEPTH - 1, -1, -1):
                    n = 1 << level
                    w = (LEAVES // 2) // n
                    left = cur[:, 0:count, :].rearrange("p t (n w) -> p t n w", w=w)[:, :, :, 0]
                    if level == DEPTH - 1:
                        take = odd
                    else:
                        take = cur[:, 0:count, :].rearrange("p t (n w) -> p t n w", w=w)[:, :, :, w // 2]
                    link(nc.vector.copy_predicated(left, right[:, 0:count, n - 1:2 * n - 1], take))
                return nc.vector.tensor_copy(idx[:, first:first + count], cur[:, 0:count, 0])

            def hidden_layer(b, t):
                lf = leaf[t % 2]
                dve.wait_ge(S["prod_ready"], prods(b, t, 0))
                link(nc.vector.reduce_sum(hid[:, t, :], lf[:, 0:W1].rearrange("p (l d) -> p l d", l=LW), axis=AXX))
                if t < 3:
                    link(tt(hid[:, t, :], hid[:, t, :], lf[:, 2 * W1:2 * W1 + LW], ALU.add))
                    nc.vector.tensor_scalar_max(hid[:, t, :], hid[:, t, :], 0.0).then_inc(S["h_ready"], 1)
                else:
                    tt(hid[:, t, :], hid[:, t, :], lf[:, 2 * W1:2 * W1 + LW], ALU.add).then_inc(S["ff_pre"], 1)

            def leaf_output(b, t):
                lf = leaf[t % 2]
                dve.wait_ge(S["prod_ready"], prods(b, t, 1))
                link(nc.vector.reduce_sum(tree[:, t, :], lf[:, W1:2 * W1].rearrange("p (d l) -> p d l", l=LW),
                                          axis=AXX))
                tt(tree[:, t, :], tree[:, t, :], lf[:, 2 * W1 + LW:ROW], ALU.add).then_inc(S["leaf_taken"], 1)

            def groups(ap):
                return ap.rearrange("p (h v) -> p h v", h=RH)

            def rest(k, b):
                if k == "x1":
                    dve.wait_ge(S["proj_done"], b + 1)
                    link(tt(x1[:], ps_m[:, 0:P], x_sb[:, b, :], ALU.add))
                    statistics(x1[:], EPS, pows(b, 0))
                    nc.vector.tensor_scalar(xn1[:], x1[:], mv[:, 0, 0:1], rstd[:, 0:1], ALU.subtract, ALU.mult)\
                        .then_inc(S["xn1_ready"], 1)
                elif k == "rope":
                    dve.wait_ge(S["qk_done"], b + 1)
                    a = ps_m[:].rearrange("p (i n) -> p i n", i=4)
                    tt(qk_a[:], a[:, 0:2, :], xp[:, 0:2, :], ALU.mult).then_inc(S["dve_link"], 1)
                    links[0] += 1
                    link(tt(qk_b[:], a[:, 2:4, :], xp[:, 2:4, :], ALU.mult))
                    tt(qk_x[:], qk_a[:], qk_b[:], ALU.add).then_inc(S["qkx_ready"], 1)
                elif k == "silu":
                    dve.wait_ge(S["eg_ready"], b + 1)
                    link(nc.vector.tensor_scalar_add(silu[:], silu[:], 1.0))
                    link(nc.vector.reciprocal(silu[:], silu[:]))
                    tt(silu[:], ps_m[:, P:2 * P], silu[:], ALU.mult).then_inc(S["silu_ready"], 1)
                elif k in ("decay0", "decay1"):
                    second = int(k == "decay1")
                    dve.wait_ge(S["sc_done"], 2 * b + second + 1)
                    hs = slice(4 * second, 4 * second + 4)
                    tt(sm[:, hs, :], ps_m[:].rearrange("p (h n) -> p h n", h=4), dec[:, hs, :], ALU.mult)\
                        .then_inc(S["sm_ready"], 1)
                elif k == "norm":
                    dve.wait_ge(S["y_done"], b + 1)
                    link(nc.vector.reduce_sum(gmean[:], groups(ps_m[:, 0:P]), axis=AXX))
                    link(nc.vector.tensor_scalar_mul(gmean[:], gmean[:], 1.0 / RE))
                    bc = gmean[:].rearrange("p (h o) -> p h o", o=1).to_broadcast([P, RH, RE])
                    link(tt(groups(yc), groups(ps_m[:, 0:P]), bc, ALU.subtract))
                    link(tt(ysq, yc, yc, ALU.mult))
                    link(nc.vector.reduce_sum(gmean[:], groups(ysq), axis=AXX))
                    nc.vector.tensor_scalar(var[:], gmean[:], 1.0 / RE, EPS, ALU.mult, ALU.add)\
                        .then_inc(S["var_ready"], 1)
                    dve.wait_ge(S["rstd_ready"], pows(b, 1))
                    bc = rstd[:].rearrange("p (h o) -> p h o", o=1).to_broadcast([P, RH, RE])
                    link(tt(groups(yc), groups(yc), bc, ALU.mult))
                    link(tt(yc, yc, gn[:, 0, :], ALU.mult))
                    link(tt(yc, yc, gn[:, 1, :], ALU.add))
                    tt(yc, yc, silu[:], ALU.mult).then_inc(S["gated_ready"], 1)
                elif k == "x2":
                    dve.wait_ge(S["wo_done"], b + 1)
                    link(tt(x2[:], ps_m[:, 2 * P:3 * P], x1[:], ALU.add))
                    statistics(x2[:], EPS, pows(b, 2))
                    link(nc.vector.tensor_scalar(xl, x2[:], mv[:, 0, 0:1], rstd[:, 0:1], ALU.subtract, ALU.mult))
                    statistics(xl, 0.0, pows(b, 3), scale=D / (D - 1.0))
                    nc.vector.tensor_scalar(xf[:], xl, mv[:, 0, 0:1], rstd[:, 0:1], ALU.subtract, ALU.mult)\
                        .then_inc(S["xf_ready"], 1)
                elif k == "turns":
                    dve.wait_ge(S["lg_done"], b + 1)
                    lg = ps_m[:].rearrange("p (t n) -> p t n", t=2)[:, :, 0:NODES]
                    nc.vector.scalar_tensor_tensor(right[:, 0:2, :], nb[:, 0:2, :], -1.0, lg, ALU.mult, ALU.is_lt)\
                        .then_inc(S["mask_ready"], 1)
                elif k == "route":
                    dve.wait_ge(S["lgv_done"], b + 1)
                    dve.wait_ge(S["mask_ready"], b + 1)
                    link(nc.vector.scalar_tensor_tensor(right[:, 2, :], nb[:, 2, :], -1.0, ps_m[:, 0:NODES],
                                                        ALU.mult, ALU.is_lt))
                    route(0, 3).then_inc(S["idx_ready"], 1)
                elif k[:3] == "hid":
                    hidden_layer(b, int(k[3]))
                elif k in ("out0", "out1", "out2"):
                    leaf_output(b, int(k[3]))
                elif k == "attmax":
                    dve.wait_ge(S["at_done"], b + 1)
                    link(nc.vector.reduce_max(att_nm[:], ps_m[:, 2 * P:3 * P], axis=AXX))
                    nc.vector.tensor_scalar_mul(att_nm[:], att_nm[:], -FSCALE).then_inc(S["nm_ready"], 1)
                elif k == "y":
                    dve.wait_ge(S["ap_ready"], b + 1)
                    link(nc.vector.reciprocal(att_r[:], att_sum[:]))
                    dve.wait_ge(S["yv_done"], b + 1)
                    nc.vector.scalar_tensor_tensor(y[:], ps_m[:, 0:P], att_r[:], xf[:], ALU.mult, ALU.add)\
                        .then_inc(S["y_ready"], 1)
                elif k == "route_f":
                    dve.wait_ge(S["lgf_done"], b + 1)
                    link(nc.vector.scalar_tensor_tensor(right[:, 0, :], nb[:, 3, :], -1.0,
                                                        ps_m[:, 256:256 + NODES], ALU.mult, ALU.is_lt))
                    route(3, 1).then_inc(S["idxf_ready"], 1)
                elif k == "out3":
                    leaf_output(b, 3)
                    dve.wait_ge(S["leaf_taken"], 4 * b + 4)
                    link(tt(tree[:, 3, :], tree[:, 3, :], y[:], ALU.add))
                    if b >= 1:
                        dve.wait_ge(S["stored"], 16 * b)
                    tt(res[:], tree[:, 3, :], x2[:], ALU.add).then_inc(S["out_ready"], 1)

            dve.wait_ge(S["ld_x"], 16)
            for t in range(B):
                links[0] += 1
                nc.vector.bn_stats(st6[:, t, :], x_sb[:, t, :]).then_inc(S["dve_link"], 1)
            dve.wait_ge(S["dve_link"], links[0])
            for t in range(B):
                links[0] += 1
                nc.vector.bn_aggr(mv[:, t, :], st6[:, t, :]).then_inc(S["dve_link"], 1)
            dve.wait_ge(S["dve_link"], links[0])
            nc.vector.memset(var[:], 1.0).then_inc(S["dve_link"], 1)
            links[0] += 1
            dve.wait_ge(S["dve_link"], links[0])
            nc.vector.tensor_scalar_add(var[:, 0:B], mv[:, :, 1], EPS).then_inc(S["var_ready"], 1)
            dve.wait_ge(S["rstd_ready"], 1)
            for t in range(B):
                last = nc.vector.tensor_scalar(qmask[:, t, :], x_sb[:, t, :], mv[:, t, 0:1], rstd[:, t:t + 1],
                                               ALU.subtract, ALU.mult)
            last.then_inc(S["xn_ready"], 1)
            dve.wait_ge(S["wqk_done"], 1)
            nc.vector.tensor_scalar_mul(wqk[:].rearrange("p h d -> p (h d)")[:, 1024:2048], ps_s[:, 1024:2048], QSCALE)\
                .then_inc(S["wqk_b"], 1)
            dve.wait_ge(S["hi_done"], 1)
            tt(q_lo[:, 0, :], ps_m[:, 0:2 * P], q_hi[:, 0, :].bitcast(F32), ALU.subtract).then_inc(S["q0_ready"], 1)
            his[0] = 1

            def lower(n, g):
                i = RING[("T", n, g)]
                his[0] += 1
                dve.wait_ge(S["hi_done"], his[0])
                pp, row = part(n // 2, KPC * g)
                at = (slice(None), pp, slice(row, row + KPC), slice(P * (n % 2), P * (n % 2 + 1)))
                tt(pt_lo[at], ps_ring[:, i % 2, :].rearrange("p (k q) -> p k q", k=KPC), pt_hi[at].bitcast(F32),
                   ALU.subtract).then_inc(S["ring_free"], 1)

            def max_half(n, e):
                dve.wait_ge(S["s_done"], CH * n + 2 * e + 2)
                links[0] += 1
                nc.vector.reduce_max(chunk_max[:, n, e:e + 1], ps_s[:, 1024 * e:1024 * (e + 1)], axis=AXX)\
                    .then_inc(S["dve_link"], 1)

            for s in range(SLOTS):
                n, tr = s, s - 2
                if query_pair(s - 1) is not None:
                    i, j = RING[("X", s - 1, 0)], query_pair(s - 1) % 2
                    his[0] += 1
                    dve.wait_ge(S["hi_done"], his[0])
                    tt(q_lo[:, j, :], ps_ring[:, i % 2, 0:2 * P], q_hi[:, j, :].bitcast(F32), ALU.subtract)\
                        .then_inc(S["ring_free"], 1)
                trs = 0 <= tr < HEADS
                if trs:
                    lower(tr, 0)
                    lower(tr, 1)
                for k, b in steps_at(DVE_AT, s, 0):
                    rest(k, b)
                if n < HEADS:
                    max_half(n, 0)
                    max_half(n, 1)
                    dve.wait_ge(S["dve_link"], links[0])
                    nc.vector.tensor_reduce(neg_max[:, n:n + 1], chunk_max[:, n, :], axis=AXX, op=ALU.max,
                                            negate=True).then_inc(S["negmax_ready"], 1)
                if trs:
                    lower(tr, 2)
                    lower(tr, 3)
                if o_pair(s) is not None:
                    two = slice(2 * o_pair(s), 2 * o_pair(s) + 2)
                    dve.wait_ge(S["exp_done"], 4 * o_pair(s) + 4)
                    link(nc.vector.reduce_sum(sum_all[:, two], sums[:, two, :], axis=AXX))
                    nc.vector.reciprocal(rsum[:, two], sum_all[:, two]).then_inc(S["rsum_ready"], 1)
                for k, b in steps_at(DVE_AT, s, 1):
                    rest(k, b)

        @block.gpsimd
        def _(pool):
            links = [0]

            def link(ins):
                links[0] += 1
                ins.then_inc(S["pool_link"], 1)
                pool.wait_ge(S["pool_link"], links[0])

            def power(n, count):
                pool.wait_ge(S["var_ready"], count)
                nc.gpsimd.tensor_tensor(rstd[:, 0:n], var[:, 0:n], half[:, 0, 0:n], ALU.pow).then_inc(S["rstd_ready"], 1)

            def split_ct(i):
                b, c = i // CH, i % CH
                pool.wait_ge(S[f"ld_ct{i % 2}"], 16 * (i // 2 + 1))
                if b:
                    pool.wait_ge(S["s_done"], CH * (H * b - 1) + c + 1)
                o = slice(512 * c, 512 * (c + 1))
                link(nc.gpsimd.tensor_copy(ct_hi[:, o], ct_stage[:, i % 2, :]))
                nc.gpsimd.tensor_tensor(ct_lo[:, o], ct_stage[:, i % 2, :], ct_hi[:, o].bitcast(F32), ALU.subtract)\
                    .then_inc(S["ct_split"], 1)

            def split_c(i):
                b, c = i // CH, i % CH
                pool.wait_ge(S[f"ld_c{i % 2}"], 16 * (i // 2 + 1))
                if b:
                    pool.wait_ge(S["av_done"], 2 * PPB * b - 1 + c // 2)
                o = slice(KPC * c, KPC * (c + 1))
                link(nc.gpsimd.tensor_copy(c_hi[:, o, :], c_stage[:, i % 2, :, :]))
                nc.gpsimd.tensor_tensor(c_lo[:, o, :], c_stage[:, i % 2, :, :], c_hi[:, o, :].bitcast(F32), ALU.subtract)\
                    .then_inc(S["c_split"], 1)

            def gather(b, t):
                nc.gpsimd.indirect_dma_start(
                    out=leaf[t % 2][:], out_offset=None, in_=leaves[t],
                    in_offset=bass.IndirectOffsetOnAxis(ap=idx[:, t:t + 1], axis=0),
                ).then_inc(S[f"gather{t % 2}"], 16)

            def up(b, t):
                lf = leaf[t % 2]
                src = (xf if t < 3 else y)[:].rearrange("p (o d) -> p o d", o=1).to_broadcast([P, LW, D])
                pool.wait_ge(S[f"gather{t % 2}"], 16 * (2 * b + t // 2 + 1))
                w = lf[:, 0:W1].rearrange("p (l d) -> p l d", l=LW)
                nc.gpsimd.tensor_tensor(w, w, src, ALU.mult).then_inc(S["prod_ready"], 1)

            def down(b, t):
                lf = leaf[t % 2]
                pool.wait_ge(S["h_ready"], 4 * b + t + 1)
                w = lf[:, W1:2 * W1].rearrange("p (d l) -> p d l", l=LW)
                h = hid[:, t, :].rearrange("p (o l) -> p o l", o=1).to_broadcast([P, D, LW])
                nc.gpsimd.tensor_tensor(w, w, h, ALU.mult).then_inc(S["prod_ready"], 1)

            def rest(k, b):
                if k == "root1":
                    power(1, pows(b, 0))
                elif k == "mask_q":
                    pool.wait_ge(S["qkx_ready"], b + 1)
                    q = qk_x[:, 0:1, :].to_broadcast([P, RH, P])
                    m = hmask[:].rearrange("p (h o) -> p h o", o=1).to_broadcast([P, RH, P])
                    nc.gpsimd.tensor_tensor(qmask[:], q, m, ALU.mult).then_inc(S["qmask_ready"], 1)
                elif k == "root_n":
                    power(RH, pows(b, 1))
                elif k == "roots2":
                    power(1, pows(b, 2))
                    pool.wait_ge(S["var_ready"], pows(b, 3))
                    link(nc.gpsimd.tensor_tensor(rstd[:, 1:2], var[:, 0:1], half[:, 1, 0:1], ALU.pow))
                    link(nc.gpsimd.tensor_scalar_add(rstd[:, 2:3], rstd[:, 1:2], EPS))
                    nc.gpsimd.tensor_tensor(rstd[:, 0:1], rstd[:, 2:3], half[:, 0, 0:1], ALU.pow)\
                        .then_inc(S["rstd_ready"], 1)
                elif k == "gather01":
                    pool.wait_ge(S["idx_ready"], b + 1)
                    if b >= 1:
                        pool.wait_ge(S["leaf_taken"], 4 * b)
                    gather(b, 0)
                    gather(b, 1)
                elif k == "gather2":
                    pool.wait_ge(S["leaf_taken"], 4 * b + 1)
                    gather(b, 2)
                elif k == "gather3":
                    pool.wait_ge(S["idxf_ready"], b + 1)
                    gather(b, 3)
                elif k[:2] == "up":
                    up(b, int(k[2]))
                elif k[:4] == "down":
                    down(b, int(k[4]))

            nc.gpsimd.memset(half[:, 0, :], -0.5).then_inc(S["pool_link"], 1)
            link(nc.gpsimd.memset(half[:, 1, :], 0.5))
            links[0] += 1
            pool.wait_ge(S["pool_link"], links[0])
            power(B, 1)
            for c in range(CH):
                split_ct(c)
            for c in range(CH):
                split_c(c)
            pool.wait_ge(S["ld_rest"], 16 * 8)
            for s in range(SLOTS):
                for k, b in steps_at(POOL_AT, s, 0):
                    rest(k, b)
                if s % H == H - 1 and s // H + 1 < B:
                    for c in range(CH):
                        split_ct(CH * (s // H + 1) + c)
                if s >= H and s % H == 1 and s // H < B:
                    split_c(CH * (s // H))
                    split_c(CH * (s // H) + 1)
                if s >= H and s % H == 2 and s // H < B:
                    split_c(CH * (s // H) + 2)
                    split_c(CH * (s // H) + 3)
                for k, b in steps_at(POOL_AT, s, 1):
                    rest(k, b)


def _xpos_tables(np):
    f = np.float32
    half = RE // 2
    pos = np.arange(P, dtype=f)
    base = ((np.arange(0, RE, 2, dtype=f) + f(0.4 * RE)) / f(1.4 * RE)).astype(f)
    scale = (base[None, :] ** (pos[:, None] / f(512.0))).astype(f)
    inv_freq = (f(1.0) / f(10000.0) ** (np.arange(half, dtype=f) / f(half))).astype(f)
    ang = (pos[:, None] * inv_freq[None, :]).astype(f)
    sin, cos = np.sin(ang), np.cos(ang)
    sign = np.tile(np.array([-1.0, 1.0], f), half)
    out = []
    for trig, sg in ((cos, None), (sin, sign)):
        for sc in (scale, (f(1.0) / scale).astype(f)):
            t = np.repeat((trig * sc).astype(f), 2, axis=-1)
            t = t if sg is None else t * sg[None, :]
            out.append(np.tile(t.T, (RH, 1)))
    return np.ascontiguousarray(np.stack(out, 1).astype(f))


def _decay(np):
    f = np.float32
    lo, hi = np.log(1.0 / 32.0), np.log(1.0 / 512.0)
    gam = (f(1.0) - np.exp(np.linspace(lo, hi, RH).astype(f)).astype(f)).astype(f)
    n, m = np.arange(P)[None, :], np.arange(P)[:, None]
    e = (n - m).astype(f)[None] * np.log(gam).astype(f)[:, None, None]
    d = np.where((n >= m)[None], np.exp(np.minimum(e, 0)), 0.0).astype(f)
    return np.ascontiguousarray(d.transpose(1, 0, 2))


def kernel(**inputs):
    import numpy as np
    import concourse.bacc as bacc
    from concourse import mybir as mb
    from concourse.bass_utils import run_bass_kernel_spmd as run

    g = {k: np.asarray(v) for k, v in inputs.items()}
    heads = lambda w: w.transpose(1, 0, 2).reshape(D, RH * RE)
    swap = np.arange(D) ^ 1
    wq, wk, wv = (heads(g[f"L0_attn_W_{c}"]) for c in "QKV")
    small = np.stack([wq, wk, wq[:, swap], wk[:, swap], wv, g["L0_attn_W_G"], g["L0_attn_W_O"]], 1)
    trees = "qkvf"

    def rows(t):
        w1 = g[f"L0_ffn_{t}_w1"].transpose(0, 2, 1).reshape(LEAVES, W1)
        w2 = g[f"L0_ffn_{t}_w2"].transpose(0, 2, 1).reshape(LEAVES, W1)
        return np.concatenate([w1, w2, g[f"L0_ffn_{t}_b1"], g[f"L0_ffn_{t}_b2"]], 1)

    ids = np.arange(LEAVES, dtype=np.float32)
    arrays = {
        "x": g["x"],
        "ctx_rows": g["ctx_1024"],
        "ctx_t": g["ctx_1024"].transpose(0, 2, 1),
        "wq_t": g["L0_xattn_w_q"].T,
        "wk_t": g["L0_xattn_w_k"].T,
        "w_v": g["L0_xattn_w_v"],
        "w_o": g["L0_xattn_w_o"],
        "w_small": small,
        "xpos": _xpos_tables(np),
        "decay": _decay(np),
        "head_mask": (np.arange(P)[:, None] // RE == np.arange(RH)[None, :]).astype(np.float32),
        "gn_wb": np.stack([g["L0_attn_gn_weight"], g["L0_attn_gn_bias"]], 0),
        "node_w": np.stack([g[f"L0_ffn_{t}_nw"].T for t in trees], 1),
        "node_b": np.stack([g[f"L0_ffn_{t}_nb"] for t in trees], 0),
        **{f"leaves_{t}": rows(t) for t in trees},
        "leaf_ids": np.stack([ids[0::2], ids[1::2]], 0),
        "ident_in": np.eye(P, dtype=np.float32),
    }
    arrays = {f"{k}_dram": np.ascontiguousarray(v) for k, v in arrays.items()}
    nc = bacc.Bacc("TRN2", target_bir_lowering=False, num_devices=1)
    ap = {k[:-5]: nc.dram_tensor(k, v.shape, mb.dt.from_np(v.dtype), kind="ExternalInput").ap()
          for k, v in arrays.items()}
    out = nc.dram_tensor("out_dram", (B, P, D), mb.dt.float32, kind="ExternalOutput").ap()
    leaves = [ap.pop(f"leaves_{t}") for t in trees]
    program(nc, leaves=leaves, out=out, **ap)
    r = run(nc, [arrays], core_ids=[0])
    return r.results[0]["out_dram"]
```
